# Optimizing a Trainium2 kernel written in Bass

```python
import numpy as np
import jax
import jax.numpy as jnp

def _softmax(x, axis=-1):
    return jax.nn.softmax(x, axis=axis)

def _gelu(x):
    return jax.nn.gelu(x, approximate=True)

def _silu(x):
    return jax.nn.silu(x)

def _sigmoid(x):
    return jax.nn.sigmoid(x)

def _layernorm(x, axis=-1, eps=1e-05):
    m = jnp.mean(x, axis=axis, keepdims=True)
    v = jnp.var(x, axis=axis, keepdims=True)
    return (x - m) / jnp.sqrt(v + eps)

def _scatter_add(tgt, idx, src, axis=0):
    return tgt.at[idx].add(src)

def _segment_sum(src, seg, n):
    return jax.ops.segment_sum(src, seg, n)
kernel_name = 'mk_gnn_preln_d4_gnn_r8_96d3c5'

def setup_inputs(seed: int=0):
    np.random.seed(seed)
    _w = jnp.asarray

    def _rec_inputs():
        import jax
        import jax.numpy as jnp
        _gk = jax.random.key(seed)
        x = -0.0005121 + 1.001 * jax.random.normal(jax.random.fold_in(_gk, 1), (12500, 64), jnp.float32)
        src = jax.random.randint(jax.random.fold_in(_gk, 2), (200000,), 0, 12500, jnp.int32)
        dst = jnp.minimum((12500 * jax.random.uniform(jax.random.fold_in(_gk, 3), (200000,)) ** 2.0).astype(jnp.int32), 99999)
        _o = jnp.argsort(dst, stable=True)
        src = src[_o]
        dst = dst[_o]
        edge_attr_3 = jax.random.uniform(jax.random.fold_in(_gk, 11), (200000, 3), jnp.float32, 0.0, 0.999999)
        return (x, src, dst, edge_attr_3)
    x, src, dst, edge_attr_3 = _rec_inputs()

    def _L0_gnn_setup():
        import jax, jax.numpy as jnp
        import numpy as np
        N, E = (6250, 100000)
        C_IN, C_OUT, DIM, K = (64, 64, 3, 2)
        EPS = 1e-05

        def _spline_basis(edge_attr):
            D = edge_attr.shape[1]
            v = edge_attr * (K - 1)
            k0 = jnp.floor(v)
            frac = v - k0
            k0 = k0.astype(jnp.int32)
            bits = np.stack(np.unravel_index(np.arange(2 ** D), (2,) * D), axis=-1).astype(np.int32)
            bits_f = jnp.asarray(bits, dtype=edge_attr.dtype)
            w = jnp.where(bits_f[None] > 0, frac[:, None, :], 1.0 - frac[:, None, :])
            weights = jnp.prod(w, axis=-1)
            idx_d = jnp.clip(k0[:, None, :] + bits[None], 0, K - 1)
            radix = jnp.asarray(K ** np.arange(D), dtype=jnp.int32)
            idx = jnp.sum(idx_d * radix, axis=-1)
            return (weights, idx)
        key = jax.random.key(seed)
        k1, k2, k3, k4, k5 = jax.random.split(key, 5)
        x = jax.random.normal(k1, (N, C_IN), dtype=jnp.float32)
        edge_index = jax.random.randint(k2, (2, E), 0, N, dtype=jnp.int32)
        edge_attr = jax.random.uniform(k3, (E, DIM), dtype=jnp.float32)
        W = jax.random.normal(k4, (K ** DIM, C_IN, C_OUT), dtype=jnp.float32) * 0.05
        root = jax.random.normal(k5, (C_IN, C_OUT), dtype=jnp.float32) * 0.05
        gamma = jnp.ones((C_OUT,), dtype=jnp.float32)
        beta = jnp.zeros((C_OUT,), dtype=jnp.float32)
        return {'x': x, 'edge_attr': edge_attr, 'W': W, 'root': root, 'gamma': gamma, 'beta': beta, 'edge_index': edge_index}
    _L0_gnn_all = _L0_gnn_setup()
    _L0_gnn_in = {k: v for k, v in _L0_gnn_all.items() if k in ('W', 'root', 'gamma', 'beta')}
    del _L0_gnn_all

    def _L1_gnn_setup():
        import jax, jax.numpy as jnp
        import numpy as np
        NEG_SLOPE = 0.2
        key = jax.random.key(seed)
        ks = jax.random.split(key, 5)
        N, E, Din, Dout = (12500, 200000, 64, 64)
        x = jax.random.normal(ks[0], (N, Din), dtype=jnp.float32)
        edge_index = jax.random.randint(ks[1], (2, E), 0, N, dtype=jnp.int64)
        W_l = jax.random.normal(ks[2], (Din, Dout), dtype=jnp.float32) / np.sqrt(Din)
        W_r = jax.random.normal(ks[3], (Din, Dout), dtype=jnp.float32) / np.sqrt(Din)
        att = jax.random.normal(ks[4], (Dout,), dtype=jnp.float32) / np.sqrt(Dout)
        bias = jnp.zeros((Dout,), dtype=jnp.float32)
        return {'x': x, 'edge_index': edge_index, 'W_l': W_l, 'W_r': W_r, 'att': att, 'bias': bias}
    _L1_gnn_all = _L1_gnn_setup()
    _L1_gnn_in = {k: v for k, v in _L1_gnn_all.items() if k in ('W_l', 'W_r', 'att', 'bias')}
    del _L1_gnn_all

    def _L2_gnn_setup():
        import jax, jax.numpy as jnp
        import numpy as np
        N_NODES = 6250
        N_EDGES = 100000
        NODE_FEATS = 64
        HIDDEN = 64
        NUM_LAYERS = 3

        def gcn_conv(h, W, b, src, dst, num_nodes):
            h = h @ W
            deg = jax.ops.segment_sum(jnp.ones((src.shape[0],), h.dtype), dst, num_segments=num_nodes) + 1.0
            dinv = jax.lax.rsqrt(deg)
            norm = dinv[src] * dinv[dst]
            msg = h[src] * norm[:, None]
            agg = jax.ops.segment_sum(msg, dst, num_segments=num_nodes)
            agg = agg + h * (dinv * dinv)[:, None]
            return agg + b
        key = jax.random.key(seed)
        ks = jax.random.split(key, 2 + 2 * NUM_LAYERS)
        x = jax.random.normal(ks[0], (N_NODES, NODE_FEATS), dtype=jnp.float32)
        edge_index = jax.random.randint(ks[1], (2, N_EDGES), 0, N_NODES, dtype=jnp.int64)
        inp = {'x': x, 'edge_index': edge_index}
        in_f = NODE_FEATS
        for i in range(NUM_LAYERS):
            scale = 1.0 / np.sqrt(in_f)
            inp[f'W{i}'] = jax.random.uniform(ks[2 + 2 * i], (in_f, HIDDEN), minval=-scale, maxval=scale, dtype=jnp.float32)
            inp[f'b{i}'] = jnp.zeros((HIDDEN,), dtype=jnp.float32)
            in_f = HIDDEN
        return inp
    _L2_gnn_all = _L2_gnn_setup()
    _L2_gnn_in = {k: v for k, v in _L2_gnn_all.items() if k in ('W0', 'b0', 'W1', 'b1', 'W2', 'b2')}
    del _L2_gnn_all

    def _L3_gnn_setup():
        import jax, jax.numpy as jnp
        import numpy as np
        N_NODES = 12500
        N_EDGES = 200000
        F_IN = 64
        F_OUT = 64
        key = jax.random.key(seed)
        k1, k2, k3, k4 = jax.random.split(key, 4)
        x = jax.random.normal(k1, (N_NODES, F_IN), dtype=jnp.float32)
        edge_index = jax.random.randint(k2, (2, N_EDGES), 0, N_NODES, dtype=jnp.int64)
        lim = 1.0 / np.sqrt(2 * F_IN)
        W = jax.random.uniform(k3, (F_OUT, 2 * F_IN), minval=-lim, maxval=lim, dtype=jnp.float32)
        b = jax.random.uniform(k4, (F_OUT,), minval=-lim, maxval=lim, dtype=jnp.float32)
        return {'x': x, 'edge_index': edge_index, 'num_nodes': N_NODES, 'W': W, 'b': b}
    _L3_gnn_all = _L3_gnn_setup()
    _L3_gnn_in = {k: v for k, v in _L3_gnn_all.items() if k in ('W', 'b')}
    del _L3_gnn_all
    return {'x': x, 'src': src, 'dst': dst, 'edge_attr_3': edge_attr_3, 'L0_gnn_W': _L0_gnn_in['W'], 'L0_gnn_root': _L0_gnn_in['root'], 'L0_gnn_gamma': _L0_gnn_in['gamma'], 'L0_gnn_beta': _L0_gnn_in['beta'], 'L1_gnn_W_l': _L1_gnn_in['W_l'], 'L1_gnn_W_r': _L1_gnn_in['W_r'], 'L1_gnn_att': _L1_gnn_in['att'], 'L1_gnn_bias': _L1_gnn_in['bias'], 'L2_gnn_W0': _L2_gnn_in['W0'], 'L2_gnn_b0': _L2_gnn_in['b0'], 'L2_gnn_W1': _L2_gnn_in['W1'], 'L2_gnn_b1': _L2_gnn_in['b1'], 'L2_gnn_W2': _L2_gnn_in['W2'], 'L2_gnn_b2': _L2_gnn_in['b2'], 'L3_gnn_W': _L3_gnn_in['W'], 'L3_gnn_b': _L3_gnn_in['b']}

def reference(x, src, dst, edge_attr_3, L0_gnn_W, L0_gnn_root, L0_gnn_gamma, L0_gnn_beta, L1_gnn_W_l, L1_gnn_W_r, L1_gnn_att, L1_gnn_bias, L2_gnn_W0, L2_gnn_b0, L2_gnn_W1, L2_gnn_b1, L2_gnn_W2, L2_gnn_b2, L3_gnn_W, L3_gnn_b):
    import jax
    import jax.numpy as jnp

    def _L0_gnn_ref(x, edge_attr, W, root, gamma, beta, edge_index):
        import jax, jax.numpy as jnp
        import numpy as np
        N, E = (6250, 100000)
        C_IN, C_OUT, DIM, K = (64, 64, 3, 2)
        EPS = 1e-05

        def _spline_basis(edge_attr):
            D = edge_attr.shape[1]
            v = edge_attr * (K - 1)
            k0 = jnp.floor(v)
            frac = v - k0
            k0 = k0.astype(jnp.int32)
            bits = np.stack(np.unravel_index(np.arange(2 ** D), (2,) * D), axis=-1).astype(np.int32)
            bits_f = jnp.asarray(bits, dtype=edge_attr.dtype)
            w = jnp.where(bits_f[None] > 0, frac[:, None, :], 1.0 - frac[:, None, :])
            weights = jnp.prod(w, axis=-1)
            idx_d = jnp.clip(k0[:, None, :] + bits[None], 0, K - 1)
            radix = jnp.asarray(K ** np.arange(D), dtype=jnp.int32)
            idx = jnp.sum(idx_d * radix, axis=-1)
            return (weights, idx)
        src, dst = (edge_index[0], edge_index[1])
        Etot = edge_attr.shape[0]
        S = W.shape[0]
        weights, idx = _spline_basis(edge_attr)
        B = jnp.zeros((Etot, S), dtype=x.dtype).at[jnp.arange(Etot)[:, None], idx].add(weights)
        xj = x[src]
        z = (B[:, :, None] * xj[:, None, :]).reshape(Etot, S * x.shape[1])
        msg = z @ W.reshape(S * x.shape[1], W.shape[2])
        agg = jax.ops.segment_sum(msg, dst, num_segments=x.shape[0])
        cnt = jax.ops.segment_sum(jnp.ones((Etot,), dtype=x.dtype), dst, num_segments=x.shape[0])
        out = agg / jnp.maximum(cnt, 1.0)[:, None] + x @ root
        mean = jnp.mean(out, axis=0)
        var = jnp.var(out, axis=0)
        y = (out - mean) * jax.lax.rsqrt(var + EPS) * gamma + beta
        return jax.nn.elu(y)

    def _L1_gnn_ref(x, edge_index, W_l, W_r, att, bias):
        import jax, jax.numpy as jnp
        import numpy as np
        NEG_SLOPE = 0.2
        N = x.shape[0]
        loop = jnp.arange(N, dtype=edge_index.dtype)
        src = jnp.concatenate([edge_index[0], loop])
        dst = jnp.concatenate([edge_index[1], loop])
        x_l = x @ W_l
        x_r = x @ W_r
        e = jax.nn.leaky_relu(x_l[src] + x_r[dst], NEG_SLOPE) @ att
        e_max = jax.ops.segment_max(e, dst, num_segments=N)
        e_exp = jnp.exp(e - e_max[dst])
        denom = jax.ops.segment_sum(e_exp, dst, num_segments=N)
        alpha = e_exp / denom[dst]
        out = jax.ops.segment_sum(alpha[:, None] * x_l[src], dst, num_segments=N)
        return out + bias

    def _L2_gnn_ref(x, edge_index, W0, b0, W1, b1, W2, b2):
        import jax, jax.numpy as jnp
        import numpy as np
        N_NODES = 6250
        N_EDGES = 100000
        NODE_FEATS = 64
        HIDDEN = 64
        NUM_LAYERS = 3

        def gcn_conv(h, W, b, src, dst, num_nodes):
            h = h @ W
            deg = jax.ops.segment_sum(jnp.ones((src.shape[0],), h.dtype), dst, num_segments=num_nodes) + 1.0
            dinv = jax.lax.rsqrt(deg)
            norm = dinv[src] * dinv[dst]
            msg = h[src] * norm[:, None]
            agg = jax.ops.segment_sum(msg, dst, num_segments=num_nodes)
            agg = agg + h * (dinv * dinv)[:, None]
            return agg + b
        src, dst = (edge_index[0], edge_index[1])
        num_nodes = x.shape[0]
        h = x
        for W, b in ((W0, b0), (W1, b1), (W2, b2)):
            h = gcn_conv(h, W, b, src, dst, num_nodes)
            h = jax.nn.relu(h)
        return h

    def _L3_gnn_ref(x, edge_index, num_nodes, W, b):
        import jax, jax.numpy as jnp
        import numpy as np
        N_NODES = 12500
        N_EDGES = 200000
        F_IN = 64
        F_OUT = 64
        src = edge_index[0]
        dst = edge_index[1]
        agg = jax.ops.segment_sum(x[src], dst, num_segments=num_nodes)
        deg = jax.ops.segment_sum(jnp.ones((edge_index.shape[1],), dtype=x.dtype), dst, num_segments=num_nodes)
        agg = agg / jnp.maximum(deg, 1.0)[:, None]
        h = jnp.concatenate([agg, x], axis=-1)
        out = h @ W.T + b
        return out
    edge_index = jnp.stack([src, dst])
    h = jnp.maximum(_layernorm(x, axis=-1), 0.0)
    x = x + _L0_gnn_ref(h, edge_attr_3, L0_gnn_W, L0_gnn_root, L0_gnn_gamma, L0_gnn_beta, edge_index)
    h = jnp.maximum(_layernorm(x, axis=-1), 0.0)
    x = x + _L1_gnn_ref(h, edge_index, L1_gnn_W_l, L1_gnn_W_r, L1_gnn_att, L1_gnn_bias)
    h = jnp.maximum(_layernorm(x, axis=-1), 0.0)
    x = x + _L2_gnn_ref(h, edge_index, L2_gnn_W0, L2_gnn_b0, L2_gnn_W1, L2_gnn_b1, L2_gnn_W2, L2_gnn_b2)
    h = jnp.maximum(_layernorm(x, axis=-1), 0.0)
    x = x + _L3_gnn_ref(h, edge_index, 12500, L3_gnn_W, L3_gnn_b)
    return x

_drawn_inputs = setup_inputs


def setup_inputs(seed=0):
    import zlib

    import numpy as np

    out = dict(_drawn_inputs(seed))
    spreads = {'L0_gnn_gamma': (1.0, 0.2),
     'L0_gnn_beta': (0.0, 0.1),
     'L1_gnn_bias': (0.0, 0.1),
     'L2_gnn_b0': (0.0, 0.8),
     'L2_gnn_b1': (0.0, 0.357),
     'L2_gnn_b2': (0.0, 0.1)}
    factors = {'L1_gnn_W_r': 2.719, 'L2_gnn_W0': 3.089, 'L2_gnn_W1': 2.869}
    for name, (base, spread) in spreads.items():
        noise = np.random.default_rng([zlib.crc32(name.encode()), seed]).standard_normal(out[name].shape)
        drawn = base * np.exp(spread * noise) if base else spread * noise
        out[name] = jnp.asarray(drawn.astype(out[name].dtype))
    for name, factor in factors.items():
        out[name] = (out[name] * factor).astype(out[name].dtype)
    return out
```

```python
import concourse.bass as bass
from concourse import mybir
from contextlib import ExitStack


def gnn_stack_kernel(
    nc, x, src, dst, edge_attr, W0, root, gamma, beta, W_l, W_r, att, bias1,
    gW0, gb0, gW1, gb1, gW2, gb2, W3, b3, out,
):
    fp32 = mybir.dt.float32
    bf16 = mybir.dt.bfloat16
    i32 = mybir.dt.int32
    ALU = mybir.AluOpType
    ACT = mybir.ActivationFunctionType
    AX = mybir.AxisListType.X

    P = 128
    N, F = x.shape
    E = src.shape[0]
    D = edge_attr.shape[1]
    KS = W0.shape[0]
    T = (N + P - 1) // P
    TF = N // P
    NR = N - TF * P
    J = 4
    S = 8
    SD = 4
    GE = J * P
    NG = -(-E // (GE * S)) * S
    IT = NG // S
    NB = -(-NG * J // P)
    CH = NB * P
    EB = E // (P * P)
    ER = (E - EB * P * P) // P
    EL = E - EB * P * P - ER * P
    TG = 7
    NT = T // TG
    assert TG * NT == T and KS == 2 ** D and D == 3 and 2 * F == P
    BIG = 1.0e30
    EPS = 1e-5
    SLOPE = 0.2

    spline_tab = nc.dram_tensor("spline_tab", (T * P, F), fp32).ap()
    gat_tab = nc.dram_tensor("gat_tab", (T * P, 2 * F), fp32).ap()
    sum_tab = nc.dram_tensor("sum_tab", (T * P, 3 * F), bf16).ap()
    dst_rows = nc.dram_tensor("dst_rows", (CH * P,), fp32).ap()
    bounds_dram = nc.dram_tensor("bounds_dram", (NB * P // J * 2,), i32).ap()

    ctx = ExitStack()
    with ctx:
        def sb(name, shape, dt=fp32):
            return ctx.enter_context(nc.sbuf_tensor(name, shape, dt))

        def pb(name, cols):
            return ctx.enter_context(nc.psum_tensor(name, [P, cols], fp32))

        def sem(name):
            return ctx.enter_context(nc.semaphore(name))

        X = sb("X", [P, T * F])
        H = sb("H", [P, T * F])
        A = sb("A", [P, T * F])
        R = sb("R", [P, T * F])
        Q = sb("Q", [P, T * 3 * F], bf16)
        Xv, Hv, Av, Rv = (a[:, :].rearrange("p (t f) -> p t f", f=F) for a in (X, H, A, R))
        Qv = Q[:, :].rearrange("p (t s f) -> p t s f", s=3, f=F)

        srci = sb("srci", [P, CH], i32)
        dstf = sb("dstf", [P, CH])
        idx_ring = sb("idx_ring", [P, S * J], i32)
        gath = sb("gath", [P, S * J * P])
        bounds = sb("bounds", [1, NB * P // J * 2], i32)
        gath_spline = gath[:, :].rearrange("p (s j c) -> p s j c", s=S, j=J)[:, :, :, 0:F]
        gath_gat = gath[:, :].rearrange("p (s j c) -> p s j c", s=S, j=J)
        gath_sum = gath[:, :].bitcast(bf16).rearrange("p (s j c) -> p s j c", s=S, j=J)[:, :, :, 0:3 * F]

        ident = sb("ident", [P, P])
        ones = sb("ones", [P, P])
        iota_row = sb("iota_row", [P, P])
        tile_base = sb("tile_base", [P, T])
        node_no = sb("node_no", [P, T])
        pad_mask = sb("pad_mask", [P, 1])
        vecs = sb("vecs", [P, 8 * F])
        GAM, BET, ATT, B1, GB, B3 = 0, 1, 2, 3, 4, 7
        w_spline = sb("w_spline", [P, KS // 2 * F])
        w_root = sb("w_root", [F, F])
        w_gat = sb("w_gat", [F, 2 * F])
        w_gcn = sb("w_gcn", [F, 3 * F])
        w_cur = sb("w_cur", [F, F])
        w3_raw = sb("w3_raw", [F, 2 * F])
        w3 = sb("w3", [2 * F, F])
        att_col = sb("att_col", [P, 1])
        att_mat = sb("att_mat", [P, P])
        stage = sb("stage", [P, TG * P])
        hT = sb("hT", [P, TG * P])
        cnt = sb("cnt", [P, T])
        rdeg = sb("rdeg", [P, T])
        dinv = sb("dinv", [P, T])
        mx = sb("mx", [P, T])
        den = sb("den", [P, T])
        s1 = sb("s1", [P, T])
        s2 = sb("s2", [P, T])
        bn = sb("bn", [P, 4 * F])
        small = sb("small", [P, 8])
        cmm = sb("cmm", [P, 2 * NB])
        bnd_f = sb("bnd_f", [NB, 2 * P // J])
        bnd_i = sb("bnd_i", [NB, 2 * P // J], i32)

        raw_dst = A[:, 0:NB * P].bitcast(i32).rearrange("p (b e) -> p b e", b=NB)
        raw_src = A[:, NB * P:2 * NB * P].bitcast(i32).rearrange("p (b e) -> p b e", b=NB)
        rawf_dst = A[:, 2 * NB * P:3 * NB * P].rearrange("p (b e) -> p b e", b=NB)
        raw_att = R[:, 0:NB * P * D].rearrange("p (b e) -> p b e", b=NB)
        rawf_src = H[:, 0:NB * P].rearrange("p (b e) -> p b e", b=NB)
        wmin = H[:, NB * P:2 * NB * P].rearrange("p (b e) -> p b e", b=NB)
        hat = Q[:, 0:NG * J * D * 4].bitcast(fp32).rearrange("p (c d w) -> p c d w", d=D, w=2)
        z = R[:, 0:J * KS * F].rearrange("p (j k f) -> p j k f", j=J, k=KS)
        o = J * KS * F
        oh32 = R[:, o:o + GE].rearrange("p (j n) -> p j n", j=J)
        zt = R[:, o + GE:o + 2 * GE]
        hat2 = R[:, o + 2 * GE:o + 2 * GE + 4 * J].rearrange("p (j a b) -> p j a b", a=2, b=2)
        hat8 = R[:, o + 2 * GE + 4 * J:o + 2 * GE + 12 * J].rearrange("p (j a b) -> p j a b", a=2, b=4)
        Q32 = Q[:, :].bitcast(fp32)
        dst_bc = Q32[:, 0:SD * GE].rearrange("p (s e) -> p s e", s=SD)
        oT, neg, sT, em, pr, prT = (Q32[:, (SD + k) * GE:(SD + k + 1) * GE] for k in range(6))
        xr_t = Q32[:, (SD + 6) * GE:(SD + 6) * GE + P].rearrange("p (a f) -> p a f", a=2)
        oh16 = sb("oh16", [P, GE], bf16)
        oh16v = oh16[:, :].rearrange("p (j n) -> p j n", j=J)

        psA = pb("psA", 1024)
        psB = pb("psB", 1024)
        psC = pb("psC", 512)
        psD = pb("psD", 512)

        loaded_edges = sem("loaded_edges")
        loaded_nodes = sem("loaded_nodes")
        loaded_params = sem("loaded_params")
        raw_clear = sem("raw_clear")
        pool_const = sem("pool_const")
        pool_step = sem("pool_step")
        rows_float = sem("rows_float")
        rows_stored = sem("rows_stored")
        set_t = sem("set_t")
        set_e = sem("set_e")
        bounds_ready = sem("bounds_ready")
        bounds_stored = sem("bounds_stored")
        bounds_loaded = sem("bounds_loaded")
        link_sem = sem("link_sem")
        node_act = sem("node_act")
        node_vec = sem("node_vec")
        layer_in = sem("layer_in")
        layer_sem = sem("layer_sem")
        split_ask = sem("split_ask")
        split_done = sem("split_done")
        mask_ready = sem("mask_ready")
        att_sum = sem("att_sum")
        oh16_ready = sem("oh16_ready")
        sum16_ready = sem("sum16_ready")
        bn_ask = sem("bn_ask")
        bn_sum = sem("bn_sum")
        table_rows = sem("table_rows")
        table_ready = sem("table_ready")
        staged = sem("staged")
        prod_t = sem("prod_t")
        prod_te = sem("prod_te")
        prod_m = sem("prod_m")
        prod_me = sem("prod_me")
        w_ready = sem("w_ready")
        idx_ready = [sem(f"idx_ready{s}") for s in range(S)]
        gathered = [sem(f"gathered{s}") for s in range(S)]
        slot_free = [sem(f"slot_free{s}") for s in range(S)]
        bc_ready = [sem(f"bc_ready{s}") for s in range(SD)]
        bc_free = [sem(f"bc_free{s}") for s in range(SD)]
        hat2_ready = sem("hat2_ready")
        hat8_ready = sem("hat8_ready")
        z_ready = sem("z_ready")
        zt_ready = sem("zt_ready")
        zt_moved = sem("zt_moved")
        oh_ready = sem("oh_ready")
        sum_ready = sem("sum_ready")
        xr_ready = sem("xr_ready")
        s_ready = sem("s_ready")
        relu_ready = sem("relu_ready")
        copy_ready = sem("copy_ready")
        e_ready = sem("e_ready")
        gmax_ready = sem("gmax_ready")
        new_max = sem("new_max")
        diff_ready = sem("diff_ready")
        scale_ready = sem("scale_ready")
        p_ready = sem("p_ready")
        pT_ready = sem("pT_ready")
        pT_moved = sem("pT_moved")
        layer_done = sem("layer_done")
        out_ready = sem("out_ready")
        stored = sem("stored")

        block = ctx.enter_context(nc.Block())

        SPLINE, GAT, GCN, SAGE = 0, 1, 2, 5
        G_ROOT, G_GAT, G_GCN, G_SAGE = 0, NT, 2 * NT, 5 * NT

        def vec(k, cols=F):
            return vecs[:, k * F:k * F + cols]

        def over_tiles(ap):
            return ap.unsqueeze(1).to_broadcast([P, T, F])

        def over_features(ap):
            return ap.unsqueeze(2).to_broadcast([P, T, F])

        def wait_apart(eng, register, semaphore, target):
            eng.reg_mov(register, target)
            eng.wait_ge(loaded_edges, 16 * 9)
            eng.wait_ge(semaphore, register)

        def group_bounds(eng, i, regs):
            eng.load(regs, bounds[0:1, bass.ds(i * 2 * S, 2 * S)])

        def tiles(eng, regs, s):
            lo = eng.snap(regs[2 * s], min_val=0, max_val=T - 1)
            hi = eng.snap(regs[2 * s + 1], min_val=1, max_val=T)
            return eng.Fori(lo, hi)

        @block.sync
        def _(sp):
            sp.wait_ge(raw_clear, 1)
            for raw, lst in ((raw_dst, dst), (raw_src, src)):
                full = EB * P * P
                sp.dma_start(raw[:, 0:EB, :], lst[0:full].rearrange("(b r e) -> r b e", b=EB, r=P)).then_inc(loaded_edges, 16)
                sp.dma_start(raw[0:ER, EB, :], lst[full:full + ER * P].rearrange("(r e) -> r e", e=P)).then_inc(loaded_edges, 16)
                sp.dma_start(raw[ER:ER + 1, EB, 0:EL], lst[full + ER * P:E].rearrange("(r e) -> r e", r=1)).then_inc(loaded_edges, 16)
            ea = edge_attr.rearrange("e d -> (e d)")
            full = EB * P * P * D
            sp.dma_start(raw_att[:, 0:EB, :], ea[0:full].rearrange("(b r e) -> r b e", b=EB, r=P)).then_inc(loaded_edges, 16)
            sp.dma_start(raw_att[0:ER, EB, :], ea[full:full + ER * P * D].rearrange("(r e) -> r e", r=ER)).then_inc(loaded_edges, 16)
            sp.dma_start(raw_att[ER:ER + 1, EB, 0:EL * D], ea[full + ER * P * D:E * D].rearrange("(r e) -> r e", r=1)).then_inc(loaded_edges, 16)
            sp.dma_start(Xv[:, 0:TF, :], x[0:TF * P, :].rearrange("(t p) f -> p t f", p=P)).then_inc(loaded_nodes, 16)
            sp.dma_start(Xv[0:NR, TF, :], x[TF * P:N, :]).then_inc(loaded_nodes, 16)
            sp.wait_ge(rows_float, 1)
            sp.dma_start(dst_rows.rearrange("(b r e) -> r b e", b=NB, r=P), rawf_dst).then_inc(rows_stored, 16)
            sp.wait_ge(bounds_ready, 1)
            sp.dma_start(bounds_dram.rearrange("(b g) -> b g", b=NB), bnd_i[:, :]).then_inc(bounds_stored, 16)
            sp.wait_ge(bounds_stored, 16)
            sp.dma_start(bounds[:, :], bounds_dram.rearrange("(a g) -> a g", a=1)).then_inc(bounds_loaded, 16)

            def edge_pass(done, with_dst=False):
                with sp.Fori(0, IT) as i:
                    for s in range(S):
                        sp.wait_ge(slot_free[s], i + (done + 1))
                        sp.dma_start(idx_ring[:, s * J:(s + 1) * J],
                                     srci[:, bass.ds(i * (S * J) + s * J, J)]).then_inc(idx_ready[s], 16)
                        if with_dst:
                            sp.wait_ge(bc_free[s % SD], i * (S // SD) + (s // SD + 1))
                            row = dst_rows[bass.ds(i * (S * GE) + s * GE, GE)]
                            sp.dma_start(dst_bc[:, s % SD, :],
                                         row.rearrange("(a e) -> a e", a=1).to_broadcast([P, GE])).then_inc(bc_ready[s % SD], 16)

            sp.wait_ge(table_rows, 1)
            sp.dma_start(spline_tab.rearrange("(t p) f -> p t f", p=P), Hv).then_inc(table_ready, 16)
            edge_pass(SPLINE * IT)
            sp.wait_ge(table_rows, 2)
            rows = gat_tab.rearrange("(t p) (a f) -> p t a f", p=P, a=2)
            for a in range(2):
                sp.dma_start(rows[:, :, a, :], Av).then_inc(table_ready, 16)
            sp.wait_ge(rows_stored, 16)
            edge_pass(GAT * IT, with_dst=True)
            split_rows = sum_tab.rearrange("(t p) c -> p t c", p=P)
            Qrows = Q[:, :].rearrange("p (t c) -> p t c", t=T)
            with sp.Fori(0, 3) as layer:
                sp.wait_ge(table_rows, layer + 3)
                sp.dma_start(split_rows, Qrows).then_inc(table_ready, 16)
                edge_pass(layer * IT + GCN * IT)
            sp.wait_ge(table_rows, 6)
            sp.dma_start(split_rows, Qrows).then_inc(table_ready, 16)
            edge_pass(SAGE * IT)
            sp.wait_ge(out_ready, 1)
            sp.dma_start(out[0:TF * P, :].rearrange("(t p) f -> p t f", p=P), Xv[:, 0:TF, :]).then_inc(stored, 16)
            sp.dma_start(out[TF * P:N, :], Xv[0:NR, TF, :]).then_inc(stored, 16)
            sp.wait_ge(stored, 32)

        @block.gpsimd
        def _(pool):
            nc.gpsimd.memset(ident[:, :], 0.0).then_inc(pool_step, 1)
            nc.gpsimd.memset(ones[:, :], 1.0).then_inc(pool_step, 1)
            nc.gpsimd.iota(iota_row[:, :], [[1, P]], base=0, channel_multiplier=0,
                           allow_small_or_imprecise_dtypes=True).then_inc(pool_step, 1)
            nc.gpsimd.iota(tile_base[:, :], [[P, T]], base=0, channel_multiplier=0,
                           allow_small_or_imprecise_dtypes=True).then_inc(pool_step, 1)
            nc.gpsimd.iota(node_no[:, :], [[P, T]], base=0, channel_multiplier=1,
                           allow_small_or_imprecise_dtypes=True).then_inc(pool_step, 1)
            pool.wait_ge(pool_step, 5)
            nc.gpsimd.affine_select(out=ident[:, :], in_=ident[:, :], compare_op=ALU.not_equal, fill=1.0,
                                    base=0, pattern=[[-1, P]], channel_multiplier=1).then_inc(pool_const, 1)

            pool_count = pool.alloc_register("pool_count")

            def edge_pass(table, dest, done, tables_stored):
                wait_apart(pool, pool_count, table_ready, tables_stored)
                with pool.Fori(0, IT) as i:
                    for s in range(S):
                        wait_apart(pool, pool_count, idx_ready[s], (i + done + 1) * 16)
                        for j in range(J):
                            nc.gpsimd.indirect_dma_start(
                                out=dest[:, s, j, :], out_offset=None, in_=table,
                                in_offset=bass.IndirectOffsetOnAxis(ap=idx_ring[:, s * J + j:s * J + j + 1], axis=0),
                            ).then_inc(gathered[s], 16)

            edge_pass(spline_tab, gath_spline, SPLINE * IT, 16)
            edge_pass(gat_tab, gath_gat, GAT * IT, 48)
            with pool.Fori(0, 3) as layer:
                edge_pass(sum_tab, gath_sum, layer * IT + GCN * IT, layer * 16 + 64)
            edge_pass(sum_tab, gath_sum, SAGE * IT, 112)

        @block.scalar
        def _(act):
            def bc(v, n=F):
                return v.rearrange("(a f) -> a f", a=1).to_broadcast([P, n])

            for k, v in ((GAM, gamma), (BET, beta), (ATT, att), (B1, bias1), (GB, gb0), (GB + 1, gb1), (GB + 2, gb2), (B3, b3)):
                act.dma_start(vec(k), bc(v)).then_inc(loaded_params, 16)
            act.dma_start(w_spline[:, :].rearrange("p (k o) -> p k o", o=F),
                          W0.rearrange("(k s) c o -> (s c) k o", s=2)).then_inc(loaded_params, 16)
            act.dma_start(w_root[:, :], root).then_inc(loaded_params, 16)
            act.dma_start(w_gat[:, 0:F], W_l).then_inc(loaded_params, 16)
            act.dma_start(w_gat[:, F:2 * F], W_r).then_inc(loaded_params, 16)
            for k, w in enumerate((gW0, gW1, gW2)):
                act.dma_start(w_gcn[:, k * F:(k + 1) * F], w).then_inc(loaded_params, 16)
            act.dma_start(w3_raw[:, :], W3).then_inc(loaded_params, 16)
            for a in range(2):
                act.dma_start(att_col[a * F:(a + 1) * F, :], att.rearrange("(f a) -> f a", a=1)).then_inc(loaded_params, 16)

            steps = [0]

            def node_step(src_ap, dst_ap, func):
                steps[0] += 1
                act.wait_ge(node_vec, steps[0])
                nc.scalar.activation(dst_ap, src_ap, func).then_inc(node_act, 1)

            def layernorm_steps():
                node_step(R[:, :], H[:, :], ACT.Square)
                node_step(s2[:, :], s2[:, :], ACT.Sqrt)

            def stage_tiles(parts, first):
                K = sum(p.shape[2] for p in parts)
                to = stage[:, 0:TG * K].rearrange("p (t k) -> p t k", k=K)
                with act.Fori(0, NT) as i:
                    act.wait_ge(prod_t, i + (first + 1))
                    at = 0
                    for part in parts:
                        k = part.shape[2]
                        nc.scalar.activation(to[:, :, at:at + k], part[:, bass.ds(i * TG, TG), :], ACT.Copy).then_inc(staged, 1)
                        at += k

            regs = [act.alloc_register(f"act_bound{k}") for k in range(2 * S)]
            visit = act.alloc_register("act_visit")
            act.reg_mov(visit, 0)

            layernorm_steps()
            act.wait_ge(bounds_loaded, 16)
            with act.Fori(0, IT) as i:
                group_bounds(act, i, regs)
                for s in range(S):
                    with tiles(act, regs, s):
                        act.reg_add(visit, visit, 1)
                        act.wait_ge(zt_ready, visit)
                        nc.scalar.activation(zt, psA[:, 0:GE], ACT.Copy).then_inc(zt_moved, 1)
            node_step(s2[:, :], s2[:, :], ACT.Sqrt)
            stage_tiles([Hv], G_ROOT)
            node_step(A[:, :], H[:, :], ACT.Square)
            node_step(bn[:, 3 * F:4 * F], bn[:, 3 * F:4 * F], ACT.Sqrt)
            node_step(H[:, :], H[:, :], ACT.Exp)
            layernorm_steps()
            act.wait_ge(layer_in, 1)
            stage_tiles([Hv], G_GAT)
            act.reg_mov(visit, 0)
            with act.Fori(0, IT) as i:
                group_bounds(act, i, regs)
                for s in range(S):
                    with tiles(act, regs, s) as t:
                        act.reg_add(visit, visit, 1)
                        act.wait_ge(mask_ready, visit)
                        nc.scalar.activation(xr_t, Rv[:, bass.ds(t, 1), :].to_broadcast([P, 2, F]), ACT.Copy).then_inc(xr_ready, 1)
                        act.wait_ge(s_ready, visit)
                        nc.scalar.activation(sT[0:F, :], psA[0:F, 0:GE], ACT.Relu).then_inc(relu_ready, 1)
                        act.wait_ge(diff_ready, visit)
                        nc.scalar.activation(small[:, 3:4], small[:, 2:3], ACT.Exp).then_inc(scale_ready, 1)
                        nc.scalar.activation(pr, em, ACT.Exp, bias=small[:, 1:2], accum_out=small[:, 4:5]).then_inc(p_ready, 1)
                        act.wait_ge(pT_ready, visit)
                        nc.scalar.activation(prT, psC[:, 0:GE], ACT.Copy).then_inc(pT_moved, 1)
            layernorm_steps()
            with act.Fori(0, 3) as layer:
                act.wait_ge(layer_in, layer + 2)
                stage_tiles([Hv], layer * NT + G_GCN)
                act.wait_ge(split_ask, layer * 2 + 1)
                nc.scalar.activation(Qv[:, :, 0, :], Rv, ACT.Copy).then_inc(split_done, 1)
                act.wait_ge(split_ask, layer * 2 + 2)
                nc.scalar.activation(Qv[:, :, 1, :], Hv, ACT.Copy).then_inc(split_done, 1)
            layernorm_steps()
            node_step(Hv, Qv[:, :, 0, :], ACT.Copy)
            node_step(Rv, Qv[:, :, 1, :], ACT.Copy)
            act.wait_ge(layer_in, 6)
            stage_tiles([Av, Hv], G_SAGE)

        @block.tensor
        def _(pe):
            pe.wait_ge(pool_const, 1)
            pe.wait_ge(rows_float, 1)
            jobs = [(rawf_dst[:, b, :], P) for b in range(NB)] + [(rawf_src[:, b, :], P) for b in range(NB)]
            for d in range(D):
                jobs += [(raw_att[:, b, d::D], P) for b in range(NB)]
            for n, (rows, k) in enumerate(jobs):
                if n >= 2:
                    pe.wait_ge(set_e, n - 1)
                nc.tensor.transpose(psA[:, (n % 2) * 512:(n % 2) * 512 + P], rows, ident[:, :]).then_inc(set_t, 1)
            nc.tensor.transpose(psB[0:NB, 0:P], cmm[:, 0:NB], ident[:, :]).then_inc(set_t, 1)
            nc.tensor.transpose(psB[0:NB, 512:512 + P], cmm[:, NB:2 * NB], ident[:, :]).then_inc(set_t, 1)
            pe.wait_ge(loaded_params, 16 * 18)
            nc.tensor.transpose(psC[:, 0:F], w3_raw[:, :], ident[0:F, 0:F]).then_inc(set_t, 1)

            pe_count = pe.alloc_register("pe_count")

            def product(K, w, NW, first, parts=1, staged_before=None):
                with pe.Fori(0, NT) as i:
                    wait_apart(pe, pe_count, staged, i * parts + (staged_before + parts))
                    for k in range(TG):
                        ins = nc.tensor.transpose(psA[0:K, k * P:(k + 1) * P], stage[:, k * K:(k + 1) * K], ident[:, :])
                    ins.then_inc(prod_t, 1)
                    pe.wait_ge(prod_te, i + (first + 1))
                    for k in range(TG):
                        ins = nc.tensor.matmul(psB[:, k * NW:(k + 1) * NW], hT[0:K, k * P:(k + 1) * P], w, start=True, stop=True)
                    ins.then_inc(prod_m, 1)

            regs = [pe.alloc_register(f"pe_bound{k}") for k in range(2 * S)]
            visit = pe.alloc_register("pe_visit")
            pe.reg_mov(visit, 0)
            pe.wait_ge(bounds_loaded, 16)
            with pe.Fori(0, IT) as i:
                group_bounds(pe, i, regs)
                for s in range(S):
                    pe.wait_ge(z_ready, i * S + (s + 1))
                    with tiles(pe, regs, s):
                        pe.reg_add(visit, visit, 1)
                        pe.wait_ge(oh_ready, visit)
                        for k in range(KS // 2):
                            for j in range(J):
                                ins = nc.tensor.matmul(psA[:, k * P:(k + 1) * P], z[:, j, 2 * k:2 * k + 2, :].rearrange("p a f -> p (a f)"),
                                                       oh32[:, j, :], start=(j == 0), stop=(j == J - 1))
                        ins.then_inc(zt_ready, 1)
                        for j in range(J):
                            nc.tensor.matmul(psC[:, 0:1], oh32[:, j, :], ones[:, 0:1], start=(j == 0), stop=(j == J - 1))
                        pe.wait_ge(zt_moved, visit)
                        for k in range(KS // 2):
                            ins = nc.tensor.matmul(psD[:, 0:F], zt[:, k * P:(k + 1) * P], w_spline[:, k * F:(k + 1) * F],
                                                   start=(k == 0), stop=(k == KS // 2 - 1))
                        ins.then_inc(sum_ready, 1)
            product(F, w_root[:, :], F, G_ROOT, staged_before=0)
            for n in range(2):
                pe.wait_ge(bn_ask, n + 1)
                nc.tensor.matmul(psC[:, 0:F], ones[:, :], bn[:, n * F:(n + 1) * F], start=True, stop=True).then_inc(bn_sum, 1)
            product(F, w_gat[:, :], 2 * F, G_GAT, staged_before=NT)
            pe.reg_mov(visit, 0)
            with pe.Fori(0, IT) as i:
                group_bounds(pe, i, regs)
                for s in range(S):
                    pe.wait_ge(gathered[s], (i + (GAT * IT + 1)) * (16 * J))
                    with tiles(pe, regs, s):
                        pe.reg_add(visit, visit, 1)
                        pe.wait_ge(xr_ready, visit)
                        nc.tensor.matmul(psA[:, 0:GE], xr_t.rearrange("p a f -> p (a f)"), oT, start=True, stop=False)
                        for j in range(J):
                            ins = nc.tensor.matmul(psA[:, j * P:(j + 1) * P], gath_gat[:, s, j, :], ident[:, :], start=False, stop=(j == J - 1))
                        ins.then_inc(s_ready, 1)
                        pe.wait_ge(relu_ready, visit)
                        pe.wait_ge(copy_ready, visit)
                        nc.tensor.matmul(psB[:, 0:GE], att_mat[:, :], sT, start=True, stop=True).then_inc(e_ready, 1)
                        pe.wait_ge(p_ready, visit)
                        for j in range(J):
                            ins = nc.tensor.transpose(psC[:, j * P:(j + 1) * P], pr[:, j * P:(j + 1) * P], ident[:, :])
                        ins.then_inc(pT_ready, 1)
                        pe.wait_ge(pT_moved, visit)
                        for j in range(J):
                            ins = nc.tensor.matmul(psD[:, 0:F], prT[:, j * P:(j + 1) * P], gath_gat[:, s, j, 0:F],
                                                   start=(j == 0), stop=(j == J - 1))
                        ins.then_inc(att_sum, 1)

            pe.reg_mov(visit, 0)

            def sum_pass(done):
                with pe.Fori(0, IT) as i:
                    group_bounds(pe, i, regs)
                    for s in range(S):
                        pe.wait_ge(gathered[s], (i + done + 1) * (16 * J))
                        with tiles(pe, regs, s):
                            pe.reg_add(visit, visit, 1)
                            pe.wait_ge(oh16_ready, visit)
                            for j in range(J):
                                for part in range(3):
                                    ins = nc.tensor.matmul(psD[:, 0:F], oh16v[:, j, :], gath_sum[:, s, j, part * F:(part + 1) * F],
                                                           start=(j == 0 and part == 0), stop=(j == J - 1 and part == 2))
                            ins.then_inc(sum16_ready, 1)

            with pe.Fori(0, 3) as layer:
                wait_apart(pe, pe_count, w_ready, layer + 1)
                with pe.Fori(0, NT) as i:
                    wait_apart(pe, pe_count, staged, layer * NT + i + (2 * NT + 1))
                    for k in range(TG):
                        ins = nc.tensor.transpose(psA[0:F, k * P:(k + 1) * P], stage[:, k * F:(k + 1) * F], ident[:, :])
                    ins.then_inc(prod_t, 1)
                    pe.wait_ge(prod_te, layer * NT + i + (G_GCN + 1))
                    for k in range(TG):
                        ins = nc.tensor.matmul(psB[:, k * F:(k + 1) * F], hT[0:F, k * P:(k + 1) * P], w_cur[:, :], start=True, stop=True)
                    ins.then_inc(prod_m, 1)
                sum_pass(layer * IT + GCN * IT)
            sum_pass(SAGE * IT)
            product(2 * F, w3[:, :], F, G_SAGE, parts=2, staged_before=5 * NT)

        @block.vector
        def _(dve):
            chain = [0]

            def link(ins):
                chain[0] += 1
                ins.then_inc(link_sem, 1)
                dve.wait_ge(link_sem, chain[0])

            V = nc.vector

            V.memset(raw_dst[:, EB, :], -1)
            V.memset(raw_src[:, EB, :], 0)
            V.memset(Xv[:, TF, :], 0.0)
            V.memset(raw_att[:, EB, :], 0.0).then_inc(raw_clear, 1)
            dve.wait_ge(loaded_edges, 16 * 9)
            V.tensor_copy(rawf_src, raw_src)
            link(V.tensor_copy(rawf_dst, raw_dst))
            link(V.tensor_scalar(wmin, rawf_dst, 0.0, 2.0 * N, ALU.is_lt, ALU.mult))
            link(V.tensor_tensor(wmin, wmin, rawf_dst, ALU.add))
            V.tensor_reduce(cmm[:, 0:NB], wmin, AX, ALU.min)
            V.tensor_reduce(cmm[:, NB:2 * NB], rawf_dst, AX, ALU.max).then_inc(rows_float, 1)
            for n in range((2 + D) * NB):
                b = n % NB
                ps = psA[:, (n % 2) * 512:(n % 2) * 512 + P]
                at = slice(b * P, (b + 1) * P)
                dve.wait_ge(set_t, n + 1)
                if n < NB:
                    V.tensor_copy(dstf[:, at], ps).then_inc(set_e, 1)
                elif n < 2 * NB:
                    V.tensor_copy(srci[:, at], ps).then_inc(set_e, 1)
                else:
                    w = min(P, NG * J - b * P)
                    V.tensor_scalar(hat[:, b * P:b * P + w, n // NB - 2, 1], ps[:, 0:w], 0.0, 1.0, ALU.max, ALU.min).then_inc(set_e, 1)
            dve.wait_ge(set_e, (2 + D) * NB)
            link(V.tensor_scalar(hat[:, :, :, 0], hat[:, :, :, 1], -1.0, 1.0, ALU.mult, ALU.add))
            dve.wait_ge(set_t, (2 + D) * NB + 2)
            bf = bnd_f[:, :].rearrange("b (g w) -> b g w", w=2)
            bi = bnd_i[:, :].rearrange("b (g w) -> b g w", w=2)
            V.tensor_reduce(bf[:, :, 0], psB[0:NB, 0:P].rearrange("b (g j) -> b g j", j=J), AX, ALU.min)
            link(V.tensor_reduce(bf[:, :, 1], psB[0:NB, 512:512 + P].rearrange("b (g j) -> b g j", j=J), AX, ALU.max))
            link(V.tensor_scalar(bf[:, :, 0], bf[:, :, 0], float(T * P - 1), None, ALU.min))
            link(V.tensor_tensor(bf[:, :, 1], bf[:, :, 1], bf[:, :, 0], ALU.max))
            link(V.tensor_copy(bnd_i[:, :], bnd_f[:, :]))
            link(V.tensor_scalar(bnd_i[:, :], bnd_i[:, :], 7, None, ALU.arith_shift_right))
            V.tensor_scalar(bi[:, :, 1], bi[:, :, 1], 1, None, ALU.add).then_inc(bounds_ready, 1)
            dve.wait_ge(set_t, (2 + D) * NB + 3)
            V.tensor_copy(w3[:, :], psC[:, 0:F])
            V.tensor_scalar(att_mat[0:F, :], att_col[0:F, 0:1].to_broadcast([F, P]), 1.0 - SLOPE, None, ALU.mult)
            V.tensor_scalar(att_mat[F:P, :], att_col[F:P, 0:1].to_broadcast([F, P]), SLOPE, None, ALU.mult)
            V.tensor_scalar(pad_mask[:, :], node_no[:, T - 1:T], float(N), None, ALU.is_lt)
            link(V.memset(cnt[:, :], 0.0))
            for semaphore in slot_free + bc_free + [prod_t]:
                V.engine_nop().then_inc(semaphore, 1)

            asked = [0]

            def ask_act(ins):
                asked[0] += 1
                ins.then_inc(node_vec, 1)
                dve.wait_ge(node_act, asked[0])

            def layernorm_relu():
                link(V.tensor_reduce(s1[:, :], Xv, AX, ALU.add))
                link(V.tensor_scalar(s1[:, :], s1[:, :], 1.0 / F, None, ALU.mult))
                ask_act(V.tensor_tensor(Rv, Xv, over_features(s1[:, :]), ALU.subtract))
                link(V.tensor_reduce(s2[:, :], Hv, AX, ALU.add))
                ask_act(V.tensor_scalar(s2[:, :], s2[:, :], 1.0 / F, EPS, ALU.mult, ALU.add))
                link(V.reciprocal(s2[:, :], s2[:, :]))
                return V.scalar_tensor_tensor(Hv, Rv, 0.0, over_features(s2[:, :]), ALU.max, ALU.mult)

            regs = [dve.alloc_register(f"dve_bound{k}") for k in range(2 * S)]
            visit = dve.alloc_register("dve_visit")
            dve.reg_mov(visit, 0)

            def free_slot(s):
                V.engine_nop().then_inc(slot_free[s], 1)

            dve.wait_ge(loaded_nodes, 32)
            layernorm_relu().then_inc(table_rows, 1)
            dve.wait_ge(rows_stored, 16)
            link(V.memset(A[:, :], 0.0))

            dve.wait_ge(bounds_loaded, 16)
            with dve.Fori(0, IT) as i:
                group_bounds(dve, i, regs)
                for s in range(S):
                    col = i * (S * J) + s * J
                    h3 = hat[:, bass.ds(col, J), :, :]
                    V.tensor_tensor(hat2, h3[:, :, 1, :].unsqueeze(3).to_broadcast([P, J, 2, 2]),
                                    h3[:, :, 0, :].unsqueeze(2).to_broadcast([P, J, 2, 2]), ALU.mult).then_inc(hat2_ready, 1)
                    dve.wait_ge(hat2_ready, i * S + (s + 1))
                    V.tensor_tensor(hat8, h3[:, :, 2, :].unsqueeze(3).to_broadcast([P, J, 2, 4]),
                                    hat2.rearrange("p j a b -> p j (a b)").unsqueeze(2).to_broadcast([P, J, 2, 4]),
                                    ALU.mult).then_inc(hat8_ready, 1)
                    dve.wait_ge(hat8_ready, i * S + (s + 1))
                    dve.wait_ge(gathered[s], (i + 1) * (16 * J))
                    V.tensor_tensor(z, gath_spline[:, s, :, :].unsqueeze(2).to_broadcast([P, J, KS, F]),
                                    hat8.rearrange("p j a b -> p j (a b)").unsqueeze(3).to_broadcast([P, J, KS, F]),
                                    ALU.mult).then_inc(z_ready, 1)
                    with tiles(dve, regs, s) as t:
                        dve.reg_add(visit, visit, 1)
                        V.scalar_tensor_tensor(oh32, iota_row[:, :].unsqueeze(1).to_broadcast([P, J, P]),
                                               tile_base[:, bass.ds(t, 1)],
                                               dstf[:, bass.ds(col, J)].unsqueeze(2).to_broadcast([P, J, P]),
                                               ALU.add, ALU.is_equal).then_inc(oh_ready, 1)
                        dve.wait_ge(sum_ready, visit)
                        V.tensor_tensor(Av[:, bass.ds(t, 1), :], Av[:, bass.ds(t, 1), :], psD[:, 0:F].unsqueeze(1), ALU.add)
                        V.tensor_tensor(cnt[:, bass.ds(t, 1)], cnt[:, bass.ds(t, 1)], psC[:, 0:1], ALU.add)
                    free_slot(s)

            def product_steps(first, K, evac):
                with dve.Fori(0, NT) as i:
                    dve.wait_ge(prod_t, i + (first + 2))
                    V.tensor_copy(hT[0:K, :], psA[0:K, 0:TG * P]).then_inc(prod_te, 1)
                    dve.wait_ge(prod_m, i + first + 1)
                    evac(i)

            link(V.engine_nop())
            link(V.tensor_scalar(s1[:, :], cnt[:, :], 1.0, None, ALU.max))
            V.reciprocal(rdeg[:, :], s1[:, :])
            ask_act(V.tensor_scalar(s2[:, :], cnt[:, :], 1.0, None, ALU.add))
            V.reciprocal(dinv[:, :], s2[:, :])
            link(V.engine_nop())
            link(V.tensor_tensor(Av, Av, over_features(rdeg[:, :]), ALU.mult))

            def root_out(i):
                at = Av[:, bass.ds(i * TG, TG), :]
                V.tensor_tensor(at, at, psB[:, 0:TG * F].rearrange("p (t f) -> p t f", f=F), ALU.add)

            product_steps(G_ROOT, F, root_out)
            link(V.engine_nop())
            V.tensor_reduce(bn[:, 0:F], Av.rearrange("p t f -> p f t"), AX, ALU.add).then_inc(bn_ask, 1)
            dve.wait_ge(bn_sum, 1)
            link(V.tensor_scalar(bn[:, 2 * F:3 * F], psC[:, 0:F], 1.0 / N, None, ALU.mult))
            link(V.tensor_tensor(Av, Av, over_tiles(bn[:, 2 * F:3 * F]), ALU.subtract))
            V.tensor_scalar(Av[:, T - 1, :], Av[:, T - 1, :], pad_mask[:, 0:1], None, ALU.mult)
            ask_act(V.engine_nop())
            V.tensor_reduce(bn[:, F:2 * F], Hv.rearrange("p t f -> p f t"), AX, ALU.add).then_inc(bn_ask, 1)
            dve.wait_ge(bn_sum, 2)
            ask_act(V.tensor_scalar(bn[:, 3 * F:4 * F], psC[:, 0:F], 1.0 / N, EPS, ALU.mult, ALU.add))
            link(V.reciprocal(bn[:, 3 * F:4 * F], bn[:, 3 * F:4 * F]))
            dve.wait_ge(loaded_params, 16 * 18)
            link(V.tensor_tensor(bn[:, 3 * F:4 * F], bn[:, 3 * F:4 * F], vec(GAM), ALU.mult))
            link(V.tensor_tensor(Av, Av, over_tiles(bn[:, 3 * F:4 * F]), ALU.mult))
            link(V.tensor_tensor(Av, Av, over_tiles(vec(BET)), ALU.add))
            ask_act(V.tensor_scalar(H[:, :], A[:, :], 0.0, None, ALU.min))
            link(V.scalar_tensor_tensor(A[:, :], A[:, :], 0.0, H[:, :], ALU.max, ALU.add))
            link(V.scalar_tensor_tensor(X[:, :], A[:, :], -1.0, X[:, :], ALU.add, ALU.add))
            layernorm_relu().then_inc(layer_in, 1)

            def gat_out(i):
                ps = psB[:, 0:TG * 2 * F].rearrange("p (t a f) -> p t a f", a=2, f=F)
                V.tensor_copy(Av[:, bass.ds(i * TG, TG), :], ps[:, :, 0, :])
                V.tensor_copy(Rv[:, bass.ds(i * TG, TG), :], ps[:, :, 1, :])

            product_steps(G_GAT, F, gat_out)
            V.engine_nop().then_inc(table_rows, 1)
            link(V.engine_nop())
            link(V.tensor_tensor(H[:, :], A[:, :], R[:, :], ALU.add))
            link(V.scalar_tensor_tensor(H[:, :], H[:, :], SLOPE, H[:, :], ALU.mult, ALU.max))
            link(V.tensor_tensor(Hv, Hv, over_tiles(vec(ATT)), ALU.mult))
            V.memset(den[:, :], 1.0)
            link(V.tensor_reduce(mx[:, :], Hv, AX, ALU.add))
            dve.wait_ge(table_ready, 48)
            dve.reg_mov(visit, 0)
            with dve.Fori(0, IT) as i:
                group_bounds(dve, i, regs)
                for s in range(S):
                    dve.wait_ge(bc_ready[s % SD], (i * (S // SD) + (s // SD + 1)) * 16)
                    row = dst_bc[:, s % SD, :]
                    with tiles(dve, regs, s) as t:
                        dve.reg_add(visit, visit, 1)
                        node = node_no[:, bass.ds(t, 1)]
                        V.tensor_scalar(neg, row, node, -BIG, ALU.not_equal, ALU.mult)
                        V.tensor_scalar(oT, row, node, None, ALU.is_equal).then_inc(mask_ready, 1)
                        dve.wait_ge(s_ready, visit)
                        V.tensor_copy(sT[F:P, :], psA[F:P, 0:GE]).then_inc(copy_ready, 1)
                        dve.wait_ge(loaded_edges, 16 * 9)
                        dve.wait_ge(e_ready, visit)
                        V.tensor_tensor_reduce(out=em, in0=psB[:, 0:GE], in1=neg, scale=1.0, scalar=-3.0e38,
                                               op0=ALU.add, op1=ALU.max, accum_out=small[:, 0:1]).then_inc(gmax_ready, 1)
                        dve.wait_ge(gmax_ready, visit)
                        m_t, l_t, o_t = mx[:, bass.ds(t, 1)], den[:, bass.ds(t, 1)], Av[:, bass.ds(t, 1), :]
                        V.tensor_scalar(small[:, 1:2], small[:, 0:1], m_t, -1.0, ALU.max, ALU.mult).then_inc(new_max, 1)
                        dve.wait_ge(new_max, visit)
                        V.tensor_tensor(small[:, 2:3], m_t, small[:, 1:2], ALU.add).then_inc(diff_ready, 1)
                        dve.wait_ge(att_sum, visit)
                        V.tensor_scalar(m_t, small[:, 1:2], -1.0, None, ALU.mult)
                        V.scalar_tensor_tensor(l_t, l_t, small[:, 3:4], small[:, 4:5], ALU.mult, ALU.add)
                        V.scalar_tensor_tensor(o_t, o_t, small[:, 3:4], psD[:, 0:F].unsqueeze(1), ALU.mult, ALU.add)
                    V.engine_nop().then_inc(bc_free[s % SD], 1)
                    free_slot(s)
            link(V.engine_nop())
            link(V.reciprocal(s1[:, :], den[:, :]))
            link(V.tensor_tensor(Av, Av, over_features(s1[:, :]), ALU.mult))
            link(V.tensor_tensor(X[:, :], X[:, :], A[:, :], ALU.add))
            link(V.tensor_tensor(Xv, Xv, over_tiles(vec(B1)), ALU.add))
            layernorm_relu().then_inc(layer_in, 1)

            dve.reg_mov(visit, 0)

            def sum_pass():
                with dve.Fori(0, IT) as i:
                    group_bounds(dve, i, regs)
                    for s in range(S):
                        col = i * (S * J) + s * J
                        with tiles(dve, regs, s) as t:
                            dve.reg_add(visit, visit, 1)
                            V.scalar_tensor_tensor(oh16v, iota_row[:, :].unsqueeze(1).to_broadcast([P, J, P]),
                                                   tile_base[:, bass.ds(t, 1)],
                                                   dstf[:, bass.ds(col, J)].unsqueeze(2).to_broadcast([P, J, P]),
                                                   ALU.add, ALU.is_equal).then_inc(oh16_ready, 1)
                            dve.wait_ge(sum16_ready, visit)
                            V.tensor_tensor(Av[:, bass.ds(t, 1), :], Av[:, bass.ds(t, 1), :], psD[:, 0:F].unsqueeze(1), ALU.add)
                        free_slot(s)

            LINKS = 5
            with dve.Fori(0, 3) as layer:
                count = [0]

                def layer_link(ins):
                    count[0] += 1
                    ins.then_inc(layer_sem, 1)
                    dve.wait_ge(layer_sem, layer * LINKS + count[0])

                V.tensor_copy(w_cur[:, :], w_gcn[:, bass.ds(layer * F, F)]).then_inc(w_ready, 1)

                def gcn_out(i):
                    ps = psB[:, 0:TG * F].rearrange("p (t f) -> p t f", f=F)
                    V.tensor_tensor(Rv[:, bass.ds(i * TG, TG), :], ps,
                                    dinv[:, bass.ds(i * TG, TG)].unsqueeze(2).to_broadcast([P, TG, F]), ALU.mult)

                product_steps(layer * NT + G_GCN, F, gcn_out)
                V.engine_nop().then_inc(split_ask, 1)
                dve.wait_ge(split_done, layer * 2 + 1)
                V.tensor_tensor(Hv, Rv, Qv[:, :, 0, :], ALU.subtract).then_inc(split_ask, 1)
                dve.wait_ge(split_done, layer * 2 + 2)
                V.tensor_tensor(Qv[:, :, 2, :], Hv, Qv[:, :, 1, :], ALU.subtract).then_inc(table_rows, 1)
                V.memset(A[:, :], 0.0)
                sum_pass()
                layer_link(V.engine_nop())
                layer_link(V.tensor_tensor(A[:, :], A[:, :], R[:, :], ALU.add))
                layer_link(V.tensor_tensor(Av, Av, over_features(dinv[:, :]), ALU.mult))
                layer_link(V.tensor_tensor(Hv, Av, over_tiles(vecs[:, bass.ds(layer * F + GB * F, F)]), ALU.add))
                V.tensor_scalar(H[:, :], H[:, :], 0.0, None, ALU.max).then_inc(layer_in, 1)
                layer_link(V.engine_nop())
                assert count[0] == LINKS
            link(V.tensor_tensor(X[:, :], X[:, :], H[:, :], ALU.add))
            ask_act(layernorm_relu())
            ask_act(V.tensor_tensor(Rv, Hv, Qv[:, :, 0, :], ALU.subtract))
            V.tensor_tensor(Qv[:, :, 2, :], Rv, Qv[:, :, 1, :], ALU.subtract).then_inc(table_rows, 1)
            link(V.memset(A[:, :], 0.0))
            sum_pass()
            link(V.engine_nop())
            link(V.tensor_tensor(Xv, Xv, over_tiles(vec(B3)), ALU.add))
            V.tensor_tensor(Av, Av, over_features(rdeg[:, :]), ALU.mult).then_inc(layer_in, 1)

            def sage_out(i):
                at = Xv[:, bass.ds(i * TG, TG), :]
                V.tensor_tensor(at, at, psB[:, 0:TG * F].rearrange("p (t f) -> p t f", f=F), ALU.add)

            product_steps(G_SAGE, 2 * F, sage_out)
            V.engine_nop().then_inc(out_ready, 1)


_INS = ['x', 'src', 'dst', 'edge_attr_3', 'L0_gnn_W', 'L0_gnn_root', 'L0_gnn_gamma', 'L0_gnn_beta', 'L1_gnn_W_l',
        'L1_gnn_W_r', 'L1_gnn_att', 'L1_gnn_bias', 'L2_gnn_W0', 'L2_gnn_b0', 'L2_gnn_W1', 'L2_gnn_b1', 'L2_gnn_W2',
        'L2_gnn_b2', 'L3_gnn_W', 'L3_gnn_b']


def kernel(**inputs):
    import numpy as _np
    import concourse.bacc as _bacc
    from concourse import mybir as _mybir
    from concourse.bass_utils import run_bass_kernel_spmd as _run

    nc = _bacc.Bacc("TRN2", target_bir_lowering=False, num_devices=1)
    arrays, args = {}, []
    for name in _INS:
        a = _np.ascontiguousarray(inputs[name])
        arrays[f"in_{name}_dram"] = a
        args.append(nc.dram_tensor(f"in_{name}_dram", a.shape, _mybir.dt.from_np(a.dtype), kind="ExternalInput").ap())
    out = nc.dram_tensor("out_0_dram", inputs["x"].shape, _mybir.dt.float32, kind="ExternalOutput").ap()
    gnn_stack_kernel(nc, *args, out)
    r = _run(nc, [arrays], core_ids=[0])
    return r.results[0]["out_0_dram"]
```

```python
import concourse.bass as bass
from concourse import mybir
from contextlib import ExitStack


def gnn_stack_kernel(
    nc, x, src, dst, edge_attr, W0, root, gamma, beta, W_l, W_r, att, bias1,
    gW0, gb0, gW1, gb1, gW2, gb2, W3, b3, out,
):
    fp32 = mybir.dt.float32
    bf16 = mybir.dt.bfloat16
    fp32r = mybir.dt.float32r
    i32 = mybir.dt.int32
    ALU = mybir.AluOpType
    ACT = mybir.ActivationFunctionType
    AX = mybir.AxisListType.X

    P = 128
    N, F = x.shape
    E = src.shape[0]
    D = edge_attr.shape[1]
    KS = W0.shape[0]
    T = (N + P - 1) // P
    TF = N // P
    NR = N - TF * P
    J = 4
    S = 8
    SD = 4
    GE = J * P
    NG = -(-E // (GE * S)) * S
    IT = NG // S
    NB = -(-NG * J // P)
    CH = NB * P
    EB = E // (P * P)
    ER = (E - EB * P * P) // P
    EL = E - EB * P * P - ER * P
    TG = 7
    NT = T // TG
    assert TG * NT == T and KS == 2 ** D and D == 3 and 2 * F == P
    BIG = 1.0e30
    EPS = 1e-5
    SLOPE = 0.2

    spline_tab = nc.dram_tensor("spline_tab", (T * P, F), fp32).ap()
    gat_tab = nc.dram_tensor("gat_tab", (T * P, 2 * F), fp32).ap()
    sum_tab = nc.dram_tensor("sum_tab", (T * P, 3 * F), bf16).ap()
    dst_rows = nc.dram_tensor("dst_rows", (CH * P,), fp32).ap()
    bounds_dram = nc.dram_tensor("bounds_dram", (NB * P // J * 2,), i32).ap()

    ctx = ExitStack()
    with ctx:
        def sb(name, shape, dt=fp32):
            return ctx.enter_context(nc.sbuf_tensor(name, shape, dt))

        def pb(name, cols):
            return ctx.enter_context(nc.psum_tensor(name, [P, cols], fp32))

        def sem(name):
            return ctx.enter_context(nc.semaphore(name))

        X = sb("X", [P, T * F])
        H = sb("H", [P, T * F])
        A = sb("A", [P, T * F])
        R = sb("R", [P, T * F])
        Q = sb("Q", [P, T * 3 * F], bf16)
        Xv, Hv, Av, Rv = (a[:, :].rearrange("p (t f) -> p t f", f=F) for a in (X, H, A, R))
        Qv = Q[:, :].rearrange("p (t s f) -> p t s f", s=3, f=F)

        srci = sb("srci", [P, CH], i32)
        dstf = sb("dstf", [P, CH])
        idx_ring = sb("idx_ring", [P, S * J], i32)
        gath = sb("gath", [P, S * J * P])
        bounds = sb("bounds", [1, NB * P // J * 2], i32)
        gath_spline = gath[:, :].rearrange("p (s j c) -> p s j c", s=S, j=J)[:, :, :, 0:F]
        gath_gat = gath[:, :].rearrange("p (s j c) -> p s j c", s=S, j=J)
        gath_sum = gath[:, :].bitcast(bf16).rearrange("p (s j c) -> p s j c", s=S, j=J)[:, :, :, 0:3 * F]

        ident = sb("ident", [P, P])
        ones = sb("ones", [P, P])
        iota_row = sb("iota_row", [P, P])
        tile_base = sb("tile_base", [P, T])
        node_no = sb("node_no", [P, T])
        pad_mask = sb("pad_mask", [P, 1])
        vecs = sb("vecs", [P, 8 * F])
        GAM, BET, ATT, B1, GB, B3 = 0, 1, 2, 3, 4, 7
        w_spline = sb("w_spline", [P, KS // 2 * F])
        w_root = sb("w_root", [F, F])
        w_gat = sb("w_gat", [F, 2 * F])
        w_gcn = sb("w_gcn", [F, 3 * F])
        w_cur = sb("w_cur", [F, F])
        w3_raw = sb("w3_raw", [F, 2 * F])
        w3 = sb("w3", [2 * F, F])
        att_col = sb("att_col", [P, 1])
        att_mat = sb("att_mat", [P, P])
        stage = sb("stage", [P, TG * P])
        hT = sb("hT", [P, TG * P])
        cnt = sb("cnt", [P, T])
        rdeg = sb("rdeg", [P, T])
        dinv = sb("dinv", [P, T])
        mx = sb("mx", [P, T])
        den = sb("den", [P, T])
        s1 = sb("s1", [P, T])
        s2 = sb("s2", [P, T])
        bn = sb("bn", [P, 4 * F])
        cmm = sb("cmm", [P, 2 * NB])
        bnd_f = sb("bnd_f", [NB, 2 * P // J])
        bnd_i = sb("bnd_i", [NB, 2 * P // J], i32)

        raw_dst = A[:, 0:NB * P].bitcast(i32).rearrange("p (b e) -> p b e", b=NB)
        raw_src = A[:, NB * P:2 * NB * P].bitcast(i32).rearrange("p (b e) -> p b e", b=NB)
        rawf_dst = A[:, 2 * NB * P:3 * NB * P].rearrange("p (b e) -> p b e", b=NB)
        raw_att = R[:, 0:NB * P * D].rearrange("p (b e) -> p b e", b=NB)
        rawf_src = H[:, 0:NB * P].rearrange("p (b e) -> p b e", b=NB)
        wmin = H[:, NB * P:2 * NB * P].rearrange("p (b e) -> p b e", b=NB)
        hat = Q[:, 0:NG * J * D * 4].bitcast(fp32).rearrange("p (c d w) -> p c d w", d=D, w=2)
        z = R[:, 0:2 * J * KS * F].rearrange("p (w j c) -> p w j c", w=2, j=J)
        o = 2 * J * KS * F
        zt = R[:, o:o + GE]
        o += GE
        hat2 = R[:, o:o + 4 * J].rearrange("p (j a b) -> p j a b", a=2, b=2)
        hat8 = R[:, o + 4 * J:o + 12 * J].rearrange("p (j a b) -> p j a b", a=2, b=4)
        Q32 = Q[:, :].bitcast(fp32)
        dst_bc = Q32[:, 0:SD * GE].rearrange("p (s e) -> p s e", s=SD)
        o = SD * GE
        oT = Q32[:, o:o + 4 * GE]
        neg = Q32[:, o + 4 * GE:o + 5 * GE]
        sT = Q32[:, o + 5 * GE:o + 7 * GE]
        o += 7 * GE
        em, pr, prT = (Q32[:, o + k * GE:o + (k + 1) * GE] for k in range(3))
        xr_t = Q32[:, o + 3 * GE:o + 3 * GE + P].rearrange("p (a f) -> p a f", a=2)
        floor = sb("floor", [P, 1])
        neg_max = sb("neg_max", [P, 1])
        diff = sb("diff", [P, 1])
        gmax = sb("gmax", [P, 1])
        edge_count = sb("edge_count", [P, 4])
        decay = sb("decay", [P, 4])
        row_sum = sb("row_sum", [P, 4])
        ones_r = sb("ones_r", [P, 2], fp32r)
        one_hot = sb("one_hot", [P, GE], fp32r)
        oh32r = one_hot[:, :].rearrange("p (j n) -> p j n", j=J)
        oh32 = one_hot[:, :].bitcast(fp32).rearrange("p (j n) -> p j n", j=J)
        oh16 = sb("oh16", [P, GE], bf16)
        oh16v = oh16[:, :].rearrange("p (j n) -> p j n", j=J)

        psA = pb("psA", 1024)
        psB = pb("psB", 1024)
        psCD = pb("psCD", 1024)
        psC, psD = psCD[:, 0:512], psCD[:, 512:1024]
        psE = pb("psE", 1024)

        loaded_edges = sem("loaded_edges")
        loaded_nodes = sem("loaded_nodes")
        loaded_params = sem("loaded_params")
        raw_clear = sem("raw_clear")
        pool_const = sem("pool_const")
        pool_step = sem("pool_step")
        rows_float = sem("rows_float")
        rows_stored = sem("rows_stored")
        set_t = sem("set_t")
        set_e = sem("set_e")
        bounds_ready = sem("bounds_ready")
        bounds_stored = sem("bounds_stored")
        bounds_loaded = sem("bounds_loaded")
        link_sem = sem("link_sem")
        node_act = sem("node_act")
        node_vec = sem("node_vec")
        layer_in = sem("layer_in")
        layer_sem = sem("layer_sem")
        split_ask = sem("split_ask")
        split_done = sem("split_done")
        oh16_ready = sem("oh16_ready")
        sum16_ready = sem("sum16_ready")
        bn_ask = sem("bn_ask")
        bn_sum = sem("bn_sum")
        table_rows = sem("table_rows")
        table_ready = sem("table_ready")
        staged = sem("staged")
        prod_t = sem("prod_t")
        prod_te = sem("prod_te")
        prod_m = sem("prod_m")
        prod_me = sem("prod_me")
        w_ready = sem("w_ready")
        idx_ready = [sem(f"idx_ready{s}") for s in range(S)]
        gathered = [sem(f"gathered{s}") for s in range(S)]
        slot_free = [sem(f"slot_free{s}") for s in range(S)]
        bc_ready = [sem(f"bc_ready{s}") for s in range(SD)]
        bc_free = [sem(f"bc_free{s}") for s in range(SD)]
        hat2_ready = sem("hat2_ready")
        hat8_ready = sem("hat8_ready")
        z_ready = sem("z_ready")
        oh_ready = [sem(f"oh_ready{j}") for j in range(J)]
        oh_used = [sem(f"oh_used{j}") for j in range(J)]
        zt_ready = sem("zt_ready")
        spline_sum = sem("spline_sum")
        spline_added = sem("spline_added")
        mask_ready = sem("mask_ready")
        xr_ready = sem("xr_ready")
        s_ready = sem("s_ready")
        sT_ready = sem("sT_ready")
        e_ready = sem("e_ready")
        neg_ready = sem("neg_ready")
        gmax_ready = sem("gmax_ready")
        new_max = sem("new_max")
        diff_ready = sem("diff_ready")
        max_kept = sem("max_kept")
        p_ready = sem("p_ready")
        pT_ready = sem("pT_ready")
        pT_moved = sem("pT_moved")
        att_sum = sem("att_sum")
        att_added = sem("att_added")
        visits_init = sem("visits_init")
        layer_done = sem("layer_done")
        out_ready = sem("out_ready")
        stored = sem("stored")

        block = ctx.enter_context(nc.Block())

        SPLINE, GAT, GCN, SAGE = 0, 1, 2, 5
        G_ROOT, G_GAT, G_GCN, G_SAGE = 0, NT, 2 * NT, 5 * NT

        def vec(k, cols=F):
            return vecs[:, k * F:k * F + cols]

        def over_tiles(ap):
            return ap.unsqueeze(1).to_broadcast([P, T, F])

        def over_features(ap):
            return ap.unsqueeze(2).to_broadcast([P, T, F])

        def wait_apart(eng, register, semaphore, target):
            eng.reg_mov(register, target)
            eng.wait_ge(loaded_edges, 16 * 9)
            eng.wait_ge(semaphore, register)

        def group_bounds(eng, i, regs):
            eng.load(regs, bounds[0:1, bass.ds(i * 2 * S, 2 * S)])

        def tiles(eng, regs, s):
            lo = eng.snap(regs[2 * s], min_val=0, max_val=T - 1)
            hi = eng.snap(regs[2 * s + 1], min_val=1, max_val=T)
            return eng.Fori(lo, hi)

        def registers(eng, name, n):
            regs = [eng.alloc_register(f"{name}{k}") for k in range(n)]
            for r in regs:
                eng.reg_mov(r, 0)
            return regs

        def shift(eng, regs, value):
            for k in range(len(regs) - 1, 0, -1):
                eng.reg_mov(regs[k], regs[k - 1])
            eng.reg_mov(regs[0], value)

        def turn(eng, reg, step, size):
            eng.reg_alu(reg, reg, step, ALU.add)
            eng.reg_alu(reg, reg, size - 1, ALU.bitwise_and)

        def ring(eng, reg, width, size):
            return bass.ds(eng.snap(reg, min_val=0, max_val=size - width), width)

        LAG = 4

        @block.sync
        def _(sp):
            sp.wait_ge(raw_clear, 1)
            for raw, lst in ((raw_dst, dst), (raw_src, src)):
                full = EB * P * P
                sp.dma_start(raw[:, 0:EB, :], lst[0:full].rearrange("(b r e) -> r b e", b=EB, r=P)).then_inc(loaded_edges, 16)
                sp.dma_start(raw[0:ER, EB, :], lst[full:full + ER * P].rearrange("(r e) -> r e", e=P)).then_inc(loaded_edges, 16)
                sp.dma_start(raw[ER:ER + 1, EB, 0:EL], lst[full + ER * P:E].rearrange("(r e) -> r e", r=1)).then_inc(loaded_edges, 16)
            ea = edge_attr.rearrange("e d -> (e d)")
            full = EB * P * P * D
            sp.dma_start(raw_att[:, 0:EB, :], ea[0:full].rearrange("(b r e) -> r b e", b=EB, r=P)).then_inc(loaded_edges, 16)
            sp.dma_start(raw_att[0:ER, EB, :], ea[full:full + ER * P * D].rearrange("(r e) -> r e", r=ER)).then_inc(loaded_edges, 16)
            sp.dma_start(raw_att[ER:ER + 1, EB, 0:EL * D], ea[full + ER * P * D:E * D].rearrange("(r e) -> r e", r=1)).then_inc(loaded_edges, 16)
            sp.dma_start(Xv[:, 0:TF, :], x[0:TF * P, :].rearrange("(t p) f -> p t f", p=P)).then_inc(loaded_nodes, 16)
            sp.dma_start(Xv[0:NR, TF, :], x[TF * P:N, :]).then_inc(loaded_nodes, 16)
            sp.wait_ge(rows_float, 1)
            sp.dma_start(dst_rows.rearrange("(b r e) -> r b e", b=NB, r=P), rawf_dst).then_inc(rows_stored, 16)
            sp.wait_ge(bounds_ready, 1)
            sp.dma_start(bounds_dram.rearrange("(b g) -> b g", b=NB), bnd_i[:, :]).then_inc(bounds_stored, 16)
            sp.wait_ge(bounds_stored, 16)
            sp.dma_start(bounds[:, :], bounds_dram.rearrange("(a g) -> a g", a=1)).then_inc(bounds_loaded, 16)

            def edge_pass(done, early, with_dst=False):
                with sp.Fori(0, IT) as i:
                    for s in range(S):
                        sp.wait_ge(slot_free[s], i + (done + 1 + (early if s >= LAG else 0)))
                        sp.dma_start(idx_ring[:, s * J:(s + 1) * J],
                                     srci[:, bass.ds(i * (S * J) + s * J, J)]).then_inc(idx_ready[s], 16)
                        if with_dst:
                            sp.wait_ge(bc_free[s % SD], i * (S // SD) + (s // SD + 1))
                            row = dst_rows[bass.ds(i * (S * GE) + s * GE, GE)]
                            sp.dma_start(dst_bc[:, s % SD, :],
                                         row.rearrange("(a e) -> a e", a=1).to_broadcast([P, GE])).then_inc(bc_ready[s % SD], 16)

            sp.wait_ge(table_rows, 1)
            sp.dma_start(spline_tab.rearrange("(t p) f -> p t f", p=P), Hv).then_inc(table_ready, 16)
            edge_pass(SPLINE * IT, 1)
            sp.wait_ge(table_rows, 2)
            rows = gat_tab.rearrange("(t p) (a f) -> p t a f", p=P, a=2)
            for a in range(2):
                sp.dma_start(rows[:, :, a, :], Av).then_inc(table_ready, 16)
            sp.wait_ge(rows_stored, 16)
            edge_pass(GAT * IT, 2, with_dst=True)
            split_rows = sum_tab.rearrange("(t p) c -> p t c", p=P)
            Qrows = Q[:, :].rearrange("p (t c) -> p t c", t=T)
            with sp.Fori(0, 3) as layer:
                sp.wait_ge(table_rows, layer + 3)
                sp.dma_start(split_rows, Qrows).then_inc(table_ready, 16)
                edge_pass(layer * IT + GCN * IT, 2)
            sp.wait_ge(table_rows, 6)
            sp.dma_start(split_rows, Qrows).then_inc(table_ready, 16)
            edge_pass(SAGE * IT, 2)
            sp.wait_ge(out_ready, 1)
            sp.dma_start(out[0:TF * P, :].rearrange("(t p) f -> p t f", p=P), Xv[:, 0:TF, :]).then_inc(stored, 16)
            sp.dma_start(out[TF * P:N, :], Xv[0:NR, TF, :]).then_inc(stored, 16)
            sp.wait_ge(stored, 32)

        @block.gpsimd
        def _(pool):
            nc.gpsimd.memset(ident[:, :], 0.0).then_inc(pool_step, 1)
            nc.gpsimd.memset(ones[:, :], 1.0).then_inc(pool_step, 1)
            nc.gpsimd.iota(iota_row[:, :], [[1, P]], base=0, channel_multiplier=0,
                           allow_small_or_imprecise_dtypes=True).then_inc(pool_step, 1)
            nc.gpsimd.iota(tile_base[:, :], [[P, T]], base=0, channel_multiplier=0,
                           allow_small_or_imprecise_dtypes=True).then_inc(pool_step, 1)
            nc.gpsimd.iota(node_no[:, :], [[P, T]], base=0, channel_multiplier=1,
                           allow_small_or_imprecise_dtypes=True).then_inc(pool_step, 1)
            pool.wait_ge(pool_step, 5)
            nc.gpsimd.affine_select(out=ident[:, :], in_=ident[:, :], compare_op=ALU.not_equal, fill=1.0,
                                    base=0, pattern=[[-1, P]], channel_multiplier=1).then_inc(pool_const, 1)

            pool_count = pool.alloc_register("pool_count")

            def edge_pass(table, dest, done, tables_stored):
                wait_apart(pool, pool_count, table_ready, tables_stored)
                with pool.Fori(0, IT) as i:
                    for s in range(S):
                        wait_apart(pool, pool_count, idx_ready[s], (i + done + 1) * 16)
                        for j in range(J):
                            nc.gpsimd.indirect_dma_start(
                                out=dest[:, s, j, :], out_offset=None, in_=table,
                                in_offset=bass.IndirectOffsetOnAxis(ap=idx_ring[:, s * J + j:s * J + j + 1], axis=0),
                            ).then_inc(gathered[s], 16)

            edge_pass(spline_tab, gath_spline, SPLINE * IT, 16)
            edge_pass(gat_tab, gath_gat, GAT * IT, 48)
            with pool.Fori(0, 3) as layer:
                edge_pass(sum_tab, gath_sum, layer * IT + GCN * IT, layer * 16 + 64)
            edge_pass(sum_tab, gath_sum, SAGE * IT, 112)

        @block.scalar
        def _(act):
            def bc(v, n=F):
                return v.rearrange("(a f) -> a f", a=1).to_broadcast([P, n])

            for k, v in ((GAM, gamma), (BET, beta), (ATT, att), (B1, bias1), (GB, gb0), (GB + 1, gb1), (GB + 2, gb2), (B3, b3)):
                act.dma_start(vec(k), bc(v)).then_inc(loaded_params, 16)
            act.dma_start(w_spline[:, :].rearrange("p (k o) -> p k o", o=F),
                          W0.rearrange("(k s) c o -> (s c) k o", s=2)).then_inc(loaded_params, 16)
            act.dma_start(w_root[:, :], root).then_inc(loaded_params, 16)
            act.dma_start(w_gat[:, 0:F], W_l).then_inc(loaded_params, 16)
            act.dma_start(w_gat[:, F:2 * F], W_r).then_inc(loaded_params, 16)
            for k, w in enumerate((gW0, gW1, gW2)):
                act.dma_start(w_gcn[:, k * F:(k + 1) * F], w).then_inc(loaded_params, 16)
            act.dma_start(w3_raw[:, :], W3).then_inc(loaded_params, 16)
            for a in range(2):
                act.dma_start(att_col[a * F:(a + 1) * F, :], att.rearrange("(f a) -> f a", a=1)).then_inc(loaded_params, 16)

            steps = [0]

            def node_step(src_ap, dst_ap, func):
                steps[0] += 1
                act.wait_ge(node_vec, steps[0])
                nc.scalar.activation(dst_ap, src_ap, func).then_inc(node_act, 1)

            def layernorm_steps():
                node_step(R[:, :], H[:, :], ACT.Square)
                node_step(s2[:, :], s2[:, :], ACT.Sqrt)

            def stage_tiles(parts, first):
                K = sum(p.shape[2] for p in parts)
                to = stage[:, 0:TG * K].rearrange("p (t k) -> p t k", k=K)
                with act.Fori(0, NT) as i:
                    act.wait_ge(prod_t, i + (first + 1))
                    at = 0
                    for part in parts:
                        k = part.shape[2]
                        nc.scalar.activation(to[:, :, at:at + k], part[:, bass.ds(i * TG, TG), :], ACT.Copy).then_inc(staged, 1)
                        at += k

            regs = [act.alloc_register(f"act_bound{k}") for k in range(2 * S)]
            visit = act.alloc_register("act_visit")
            act.reg_mov(visit, 0)

            layernorm_steps()
            act.wait_ge(bounds_loaded, 16)
            psum_at = act.alloc_register("act_psum_at")
            act.reg_mov(psum_at, 0)
            col = act.alloc_register("act_col")
            act.reg_mov(col, 0)

            def spline_visit():
                act.reg_add(visit, visit, 1)
                old = ring(act, psum_at, GE, 2 * GE)
                act.wait_ge(spline_sum, visit)
                nc.scalar.activation(edge_count[:, ring(act, col, 1, 4)], psE[:, ring(act, psum_at, 1, GE + 1)], ACT.Copy)
                nc.scalar.activation(zt, psA[:, old], ACT.Copy).then_inc(zt_ready, 1)
                turn(act, psum_at, GE, 2 * GE)
                turn(act, col, 1, 4)

            with act.Fori(0, IT) as i:
                group_bounds(act, i, regs)
                for s in range(S):
                    with tiles(act, regs, s):
                        spline_visit()
            with act.Fori(0, 2):
                spline_visit()
            node_step(s2[:, :], s2[:, :], ACT.Sqrt)
            stage_tiles([Hv], G_ROOT)
            node_step(A[:, :], H[:, :], ACT.Square)
            node_step(bn[:, 3 * F:4 * F], bn[:, 3 * F:4 * F], ACT.Sqrt)
            node_step(H[:, :], H[:, :], ACT.Exp)
            layernorm_steps()
            act.wait_ge(layer_in, 1)
            stage_tiles([Hv], G_GAT)
            act.reg_mov(visit, 0)
            old_at = act.alloc_register("act_old_at")
            act.reg_mov(old_at, 0)
            act.reg_mov(col, 3)

            def gat_visit(t):
                act.reg_add(visit, visit, 1)
                act.wait_ge(mask_ready, visit)
                act.wait_ge(s_ready, visit)
                nc.scalar.activation(xr_t, Rv[:, bass.ds(t, 1), :].to_broadcast([P, 2, F]), ACT.Copy).then_inc(xr_ready, 1)
                act.wait_ge(pT_ready, visit)
                nc.scalar.activation(prT, psC[:, 0:GE], ACT.Copy).then_inc(pT_moved, 1)
                act.wait_ge(diff_ready, visit)
                c = ring(act, col, 1, 4)
                nc.scalar.activation(decay[:, c], diff[:, :], ACT.Exp)
                nc.scalar.activation(pr, em, ACT.Exp, bias=neg_max[:, :], accum_out=row_sum[:, c]).then_inc(p_ready, 1)
                nc.scalar.activation(neg, oT[:, ring(act, old_at, GE, 4 * GE)], ACT.Copy, bias=-BIG, scale=BIG).then_inc(neg_ready, 1)
                turn(act, old_at, GE, 4 * GE)
                turn(act, col, 1, 4)

            with act.Fori(0, IT) as i:
                group_bounds(act, i, regs)
                for s in range(S):
                    with tiles(act, regs, s) as t:
                        gat_visit(t)
            with act.Fori(0, LAG) as t:
                gat_visit(t)
            layernorm_steps()
            with act.Fori(0, 3) as layer:
                act.wait_ge(layer_in, layer + 2)
                stage_tiles([Hv], layer * NT + G_GCN)
                act.wait_ge(split_ask, layer * 2 + 1)
                nc.scalar.activation(Qv[:, :, 0, :], Rv, ACT.Copy).then_inc(split_done, 1)
                act.wait_ge(split_ask, layer * 2 + 2)
                nc.scalar.activation(Qv[:, :, 1, :], Hv, ACT.Copy).then_inc(split_done, 1)
            layernorm_steps()
            node_step(Hv, Qv[:, :, 0, :], ACT.Copy)
            node_step(Rv, Qv[:, :, 1, :], ACT.Copy)
            act.wait_ge(layer_in, 6)
            stage_tiles([Av, Hv], G_SAGE)

        @block.tensor
        def _(pe):
            pe.wait_ge(pool_const, 1)
            pe.wait_ge(rows_float, 1)
            jobs = [(rawf_dst[:, b, :], P) for b in range(NB)] + [(rawf_src[:, b, :], P) for b in range(NB)]
            for d in range(D):
                jobs += [(raw_att[:, b, d::D], P) for b in range(NB)]
            for n, (rows, k) in enumerate(jobs):
                if n >= 2:
                    pe.wait_ge(set_e, n - 1)
                nc.tensor.transpose(psA[:, (n % 2) * 512:(n % 2) * 512 + P], rows, ident[:, :]).then_inc(set_t, 1)
            nc.tensor.transpose(psB[0:NB, 0:P], cmm[:, 0:NB], ident[:, :]).then_inc(set_t, 1)
            nc.tensor.transpose(psB[0:NB, 512:512 + P], cmm[:, NB:2 * NB], ident[:, :]).then_inc(set_t, 1)
            pe.wait_ge(loaded_params, 16 * 18)
            nc.tensor.transpose(psC[:, 0:F], w3_raw[:, :], ident[0:F, 0:F]).then_inc(set_t, 1)

            pe_count = pe.alloc_register("pe_count")

            def product(K, w, NW, first, parts=1, staged_before=None):
                with pe.Fori(0, NT) as i:
                    wait_apart(pe, pe_count, staged, i * parts + (staged_before + parts))
                    for k in range(TG):
                        ins = nc.tensor.transpose(psA[0:K, k * P:(k + 1) * P], stage[:, k * K:(k + 1) * K], ident[:, :])
                    ins.then_inc(prod_t, 1)
                    pe.wait_ge(prod_te, i + (first + 1))
                    for k in range(TG):
                        ins = nc.tensor.matmul(psB[:, k * NW:(k + 1) * NW], hT[0:K, k * P:(k + 1) * P], w, start=True, stop=True)
                    ins.then_inc(prod_m, 1)

            regs = [pe.alloc_register(f"pe_bound{k}") for k in range(2 * S)]
            visit = pe.alloc_register("pe_visit")
            pe.reg_mov(visit, 0)
            pe.wait_ge(bounds_loaded, 16)
            psum_at, sum_at = (pe.alloc_register(f"pe_{n}") for n in ("psum_at", "sum_at"))
            pe.reg_mov(psum_at, GE)
            pe.reg_mov(sum_at, 0)

            def spline_visit(w):
                pe.reg_add(visit, visit, 1)
                first = pe.snap(psum_at, min_val=0, max_val=GE)
                count = ring(pe, psum_at, 2, GE + 2)
                done = ring(pe, sum_at, F, GE + F)
                for k in range(KS // 2):
                    block = psA[:, bass.ds(first + k * P, P)]
                    for j in range(J):
                        if k == 0:
                            pe.wait_ge(oh_ready[j], visit)
                        nc.tensor.matmul(block, z[:, w, j, k * P:(k + 1) * P], oh32[:, j, :],
                                         start=(j == 0), stop=(j == J - 1))
                        if k == KS // 2 - 1:
                            nc.tensor.matmul(psE[:, count], oh32r[:, j, :], ones_r[:, :], start=(j == 0),
                                             stop=(j == J - 1)).then_inc(oh_used[j], 1)
                pe.wait_ge(zt_ready, visit)
                for k in range(KS // 2):
                    ins = nc.tensor.matmul(psCD[:, done], zt[:, k * P:(k + 1) * P], w_spline[:, k * F:(k + 1) * F],
                                           start=(k == 0), stop=(k == KS // 2 - 1))
                ins.then_inc(spline_sum, 1)
                turn(pe, psum_at, GE, 2 * GE)
                turn(pe, sum_at, GE, 2 * GE)

            pe.wait_ge(visits_init, 1)
            with pe.Fori(0, IT) as i:
                group_bounds(pe, i, regs)
                for s in range(S):
                    pe.wait_ge(z_ready, i * S + (s + 1))
                    with tiles(pe, regs, s):
                        spline_visit(s % 2)
            with pe.Fori(0, 2):
                spline_visit(0)
            product(F, w_root[:, :], F, G_ROOT, staged_before=0)
            for n in range(2):
                pe.wait_ge(bn_ask, n + 1)
                nc.tensor.matmul(psC[:, 0:F], ones[:, :], bn[:, n * F:(n + 1) * F], start=True, stop=True).then_inc(bn_sum, 1)
            product(F, w_gat[:, :], 2 * F, G_GAT, staged_before=NT)
            pe.reg_mov(visit, 0)
            next_visit = pe.alloc_register("pe_next_visit")
            pair_at = pe.alloc_register("pe_pair_at")
            old_at = pe.alloc_register("pe_old_at")
            onehot_at = pe.alloc_register("pe_onehot_at")
            pe.reg_mov(pair_at, GE)
            pe.reg_mov(old_at, 0)
            pe.reg_mov(onehot_at, GE)
            slots = registers(pe, "pe_slot", LAG)

            def gat_visit(s):
                pe.reg_add(visit, visit, 1)
                pe.reg_add(next_visit, visit, 1)
                shift(pe, slots, s * J * P)
                pair = ring(pe, pair_at, GE, 2 * GE)
                pe.wait_ge(p_ready, visit)
                for j in range(J):
                    ins = nc.tensor.transpose(psC[:, j * P:(j + 1) * P], pr[:, j * P:(j + 1) * P], ident[:, :])
                ins.then_inc(pT_ready, 1)
                pe.wait_ge(xr_ready, visit)
                pe.wait_ge(sT_ready, visit)
                nc.tensor.matmul(psA[:, pair], xr_t.rearrange("p a f -> p (a f)"), oT[:, ring(pe, onehot_at, GE, 4 * GE)], start=True, stop=False)
                for j in range(J):
                    o = pe.snap(pair_at, min_val=0, max_val=GE)
                    ins = nc.tensor.matmul(psA[:, bass.ds(o + j * P, P)], gath_gat[:, s, j, :], ident[:, :],
                                           start=False, stop=(j == J - 1))
                ins.then_inc(s_ready, 1)
                pe.wait_ge(sT_ready, next_visit)
                pe.wait_ge(gmax_ready, visit)
                nc.tensor.matmul(psB[:, 0:GE], att_mat[:, :], sT[:, ring(pe, old_at, GE, 2 * GE)],
                                 start=True, stop=True).then_inc(e_ready, 1)
                pe.wait_ge(pT_moved, visit)
                pe.wait_ge(att_added, visit)
                for j in range(J):
                    o = pe.snap(slots[3], min_val=0, max_val=(S - 1) * J * P)
                    ins = nc.tensor.matmul(psD[:, 0:F], prT[:, j * P:(j + 1) * P], gath[:, bass.ds(o + j * P, F)],
                                           start=(j == 0), stop=(j == J - 1))
                ins.then_inc(att_sum, 1)
                turn(pe, pair_at, GE, 2 * GE)
                turn(pe, old_at, GE, 2 * GE)
                turn(pe, onehot_at, GE, 4 * GE)

            pe.wait_ge(visits_init, 2)
            with pe.Fori(0, IT) as i:
                group_bounds(pe, i, regs)
                for s in range(S):
                    pe.wait_ge(gathered[s], (i + (GAT * IT + 1)) * (16 * J))
                    with tiles(pe, regs, s):
                        gat_visit(s)
            with pe.Fori(0, LAG):
                gat_visit(0)

            pe.reg_mov(visit, 0)

            def sum_pass(done):
                with pe.Fori(0, IT) as i:
                    group_bounds(pe, i, regs)
                    for s in range(S):
                        pe.wait_ge(gathered[s], (i + done + 1) * (16 * J))
                        with tiles(pe, regs, s):
                            pe.reg_add(visit, visit, 1)
                            pe.wait_ge(oh16_ready, visit)
                            for j in range(J):
                                for part in range(3):
                                    ins = nc.tensor.matmul(psD[:, 0:F], oh16v[:, j, :], gath_sum[:, s, j, part * F:(part + 1) * F],
                                                           start=(j == 0 and part == 0), stop=(j == J - 1 and part == 2))
                            ins.then_inc(sum16_ready, 1)

            with pe.Fori(0, 3) as layer:
                wait_apart(pe, pe_count, w_ready, layer + 1)
                with pe.Fori(0, NT) as i:
                    wait_apart(pe, pe_count, staged, layer * NT + i + (2 * NT + 1))
                    for k in range(TG):
                        ins = nc.tensor.transpose(psA[0:F, k * P:(k + 1) * P], stage[:, k * F:(k + 1) * F], ident[:, :])
                    ins.then_inc(prod_t, 1)
                    pe.wait_ge(prod_te, layer * NT + i + (G_GCN + 1))
                    for k in range(TG):
                        ins = nc.tensor.matmul(psB[:, k * F:(k + 1) * F], hT[0:F, k * P:(k + 1) * P], w_cur[:, :], start=True, stop=True)
                    ins.then_inc(prod_m, 1)
                sum_pass(layer * IT + GCN * IT)
            sum_pass(SAGE * IT)
            product(2 * F, w3[:, :], F, G_SAGE, parts=2, staged_before=5 * NT)

        @block.vector
        def _(dve):
            chain = [0]

            def link(ins):
                chain[0] += 1
                ins.then_inc(link_sem, 1)
                dve.wait_ge(link_sem, chain[0])

            V = nc.vector

            V.memset(raw_dst[:, EB, :], -1)
            V.memset(raw_src[:, EB, :], 0)
            V.memset(Xv[:, TF, :], 0.0)
            V.memset(raw_att[:, EB, :], 0.0).then_inc(raw_clear, 1)
            dve.wait_ge(loaded_edges, 16 * 9)
            V.tensor_copy(rawf_src, raw_src)
            link(V.tensor_copy(rawf_dst, raw_dst))
            link(V.tensor_scalar(wmin, rawf_dst, 0.0, 2.0 * N, ALU.is_lt, ALU.mult))
            link(V.tensor_tensor(wmin, wmin, rawf_dst, ALU.add))
            V.tensor_reduce(cmm[:, 0:NB], wmin, AX, ALU.min)
            V.tensor_reduce(cmm[:, NB:2 * NB], rawf_dst, AX, ALU.max).then_inc(rows_float, 1)
            for n in range((2 + D) * NB):
                b = n % NB
                ps = psA[:, (n % 2) * 512:(n % 2) * 512 + P]
                at = slice(b * P, (b + 1) * P)
                dve.wait_ge(set_t, n + 1)
                if n < NB:
                    V.tensor_copy(dstf[:, at], ps).then_inc(set_e, 1)
                elif n < 2 * NB:
                    V.tensor_copy(srci[:, at], ps).then_inc(set_e, 1)
                else:
                    w = min(P, NG * J - b * P)
                    V.tensor_scalar(hat[:, b * P:b * P + w, n // NB - 2, 1], ps[:, 0:w], 0.0, 1.0, ALU.max, ALU.min).then_inc(set_e, 1)
            dve.wait_ge(set_e, (2 + D) * NB)
            link(V.tensor_scalar(hat[:, :, :, 0], hat[:, :, :, 1], -1.0, 1.0, ALU.mult, ALU.add))
            dve.wait_ge(set_t, (2 + D) * NB + 2)
            bf = bnd_f[:, :].rearrange("b (g w) -> b g w", w=2)
            bi = bnd_i[:, :].rearrange("b (g w) -> b g w", w=2)
            V.tensor_reduce(bf[:, :, 0], psB[0:NB, 0:P].rearrange("b (g j) -> b g j", j=J), AX, ALU.min)
            link(V.tensor_reduce(bf[:, :, 1], psB[0:NB, 512:512 + P].rearrange("b (g j) -> b g j", j=J), AX, ALU.max))
            link(V.tensor_scalar(bf[:, :, 0], bf[:, :, 0], float(T * P - 1), None, ALU.min))
            link(V.tensor_tensor(bf[:, :, 1], bf[:, :, 1], bf[:, :, 0], ALU.max))
            link(V.tensor_copy(bnd_i[:, :], bnd_f[:, :]))
            link(V.tensor_scalar(bnd_i[:, :], bnd_i[:, :], 7, None, ALU.arith_shift_right))
            V.tensor_scalar(bi[:, :, 1], bi[:, :, 1], 1, None, ALU.add).then_inc(bounds_ready, 1)
            dve.wait_ge(set_t, (2 + D) * NB + 3)
            V.tensor_copy(w3[:, :], psC[:, 0:F])
            V.memset(floor[0:F, :], 0.0)
            V.memset(floor[F:P, :], -3.0e38)
            V.tensor_scalar(att_mat[0:F, :], att_col[0:F, 0:1].to_broadcast([F, P]), 1.0 - SLOPE, None, ALU.mult)
            V.tensor_scalar(att_mat[F:P, :], att_col[F:P, 0:1].to_broadcast([F, P]), SLOPE, None, ALU.mult)
            V.tensor_scalar(pad_mask[:, :], node_no[:, T - 1:T], float(N), None, ALU.is_lt)
            link(V.memset(cnt[:, :], 0.0))
            for semaphore in slot_free + bc_free + [prod_t]:
                V.engine_nop().then_inc(semaphore, 1)

            asked = [0]

            def ask_act(ins):
                asked[0] += 1
                ins.then_inc(node_vec, 1)
                dve.wait_ge(node_act, asked[0])

            def layernorm_relu():
                link(V.tensor_reduce(s1[:, :], Xv, AX, ALU.add))
                link(V.tensor_scalar(s1[:, :], s1[:, :], 1.0 / F, None, ALU.mult))
                ask_act(V.tensor_tensor(Rv, Xv, over_features(s1[:, :]), ALU.subtract))
                link(V.tensor_reduce(s2[:, :], Hv, AX, ALU.add))
                ask_act(V.tensor_scalar(s2[:, :], s2[:, :], 1.0 / F, EPS, ALU.mult, ALU.add))
                link(V.reciprocal(s2[:, :], s2[:, :]))
                return V.scalar_tensor_tensor(Hv, Rv, 0.0, over_features(s2[:, :]), ALU.max, ALU.mult)

            regs = [dve.alloc_register(f"dve_bound{k}") for k in range(2 * S)]
            visit = dve.alloc_register("dve_visit")
            dve.reg_mov(visit, 0)

            def free_slot(s):
                V.engine_nop().then_inc(slot_free[s], 1)

            dve.wait_ge(loaded_nodes, 32)
            layernorm_relu().then_inc(table_rows, 1)
            dve.wait_ge(rows_stored, 16)
            link(V.memset(A[:, :], 0.0))

            dve.wait_ge(bounds_loaded, 16)
            V.memset(edge_count[:, :], 0.0)
            V.tensor_copy(ones_r[:, :], ones[:, 0:2])
            for a in (psA, psCD, psE):
                V.memset(a[:, :], 0.0)
            for semaphore in oh_used + [spline_sum, spline_added]:
                V.engine_nop().then_inc(semaphore, 1)
            V.engine_nop().then_inc(visits_init, 1)
            then = registers(dve, "dve_tile", 5)
            sum_at, cnt_at = (dve.alloc_register(f"dve_{n}") for n in ("sum_at", "cnt_at"))
            dve.reg_mov(sum_at, GE)
            dve.reg_mov(cnt_at, 3)

            def spline_visit(t, chunk_col):
                dve.reg_add(visit, visit, 1)
                shift(dve, then, t)
                for j in range(J):
                    dve.wait_ge(oh_used[j], visit)
                    if chunk_col is None:
                        V.tensor_scalar(oh32r[:, j, :], iota_row[:, :], 0.0, None, ALU.mult).then_inc(oh_ready[j], 1)
                    else:
                        V.tensor_scalar(oh32r[:, j, :], iota_row[:, :], tile_base[:, bass.ds(t, 1)],
                                        dstf[:, bass.ds(chunk_col + j, 1)], ALU.add, ALU.is_equal).then_inc(oh_ready[j], 1)
                dve.wait_ge(spline_sum, visit)
                dve.wait_ge(spline_added, visit)
                u = dve.snap(then[2], min_val=0, max_val=T - 1)
                o_t, c_t = Av[:, bass.ds(u, 1), :], cnt[:, bass.ds(u, 1)]
                V.tensor_tensor(o_t, o_t, psCD[:, ring(dve, sum_at, F, GE + F)].unsqueeze(1), ALU.add)
                V.tensor_tensor(c_t, c_t, edge_count[:, ring(dve, cnt_at, 1, 4)], ALU.add).then_inc(spline_added, 1)
                turn(dve, sum_at, GE, 2 * GE)
                turn(dve, cnt_at, 1, 4)

            def give_back(s):
                free_slot((s - LAG) % S)

            with dve.Fori(0, IT) as i:
                group_bounds(dve, i, regs)
                for s in range(S):
                    col = i * (S * J) + s * J
                    h3 = hat[:, bass.ds(col, J), :, :]
                    V.tensor_tensor(hat2, h3[:, :, 1, :].unsqueeze(3).to_broadcast([P, J, 2, 2]),
                                    h3[:, :, 0, :].unsqueeze(2).to_broadcast([P, J, 2, 2]), ALU.mult).then_inc(hat2_ready, 1)
                    dve.wait_ge(hat2_ready, i * S + (s + 1))
                    V.tensor_tensor(hat8, h3[:, :, 2, :].unsqueeze(3).to_broadcast([P, J, 2, 4]),
                                    hat2.rearrange("p j a b -> p j (a b)").unsqueeze(2).to_broadcast([P, J, 2, 4]),
                                    ALU.mult).then_inc(hat8_ready, 1)
                    dve.wait_ge(hat8_ready, i * S + (s + 1))
                    dve.wait_ge(gathered[s], (i + 1) * (16 * J))
                    V.tensor_tensor(z[:, s % 2, :, :].rearrange("p j (k f) -> p j k f", f=F),
                                    gath_spline[:, s, :, :].unsqueeze(2).to_broadcast([P, J, KS, F]),
                                    hat8.rearrange("p j a b -> p j (a b)").unsqueeze(3).to_broadcast([P, J, KS, F]),
                                    ALU.mult).then_inc(z_ready, 1)
                    with tiles(dve, regs, s) as t:
                        spline_visit(t, col)
                    give_back(s)
            with dve.Fori(0, 2) as t:
                spline_visit(t, None)
            for s in range(LAG):
                give_back(s)

            def product_steps(first, K, evac):
                with dve.Fori(0, NT) as i:
                    dve.wait_ge(prod_t, i + (first + 2))
                    V.tensor_copy(hT[0:K, :], psA[0:K, 0:TG * P]).then_inc(prod_te, 1)
                    dve.wait_ge(prod_m, i + first + 1)
                    evac(i)

            link(V.engine_nop())
            link(V.tensor_scalar(s1[:, :], cnt[:, :], 1.0, None, ALU.max))
            V.reciprocal(rdeg[:, :], s1[:, :])
            ask_act(V.tensor_scalar(s2[:, :], cnt[:, :], 1.0, None, ALU.add))
            V.reciprocal(dinv[:, :], s2[:, :])
            link(V.engine_nop())
            link(V.tensor_tensor(Av, Av, over_features(rdeg[:, :]), ALU.mult))

            def root_out(i):
                at = Av[:, bass.ds(i * TG, TG), :]
                V.tensor_tensor(at, at, psB[:, 0:TG * F].rearrange("p (t f) -> p t f", f=F), ALU.add)

            product_steps(G_ROOT, F, root_out)
            link(V.engine_nop())
            V.tensor_reduce(bn[:, 0:F], Av.rearrange("p t f -> p f t"), AX, ALU.add).then_inc(bn_ask, 1)
            dve.wait_ge(bn_sum, 1)
            link(V.tensor_scalar(bn[:, 2 * F:3 * F], psC[:, 0:F], 1.0 / N, None, ALU.mult))
            link(V.tensor_tensor(Av, Av, over_tiles(bn[:, 2 * F:3 * F]), ALU.subtract))
            V.tensor_scalar(Av[:, T - 1, :], Av[:, T - 1, :], pad_mask[:, 0:1], None, ALU.mult)
            ask_act(V.engine_nop())
            V.tensor_reduce(bn[:, F:2 * F], Hv.rearrange("p t f -> p f t"), AX, ALU.add).then_inc(bn_ask, 1)
            dve.wait_ge(bn_sum, 2)
            ask_act(V.tensor_scalar(bn[:, 3 * F:4 * F], psC[:, 0:F], 1.0 / N, EPS, ALU.mult, ALU.add))
            link(V.reciprocal(bn[:, 3 * F:4 * F], bn[:, 3 * F:4 * F]))
            dve.wait_ge(loaded_params, 16 * 18)
            link(V.tensor_tensor(bn[:, 3 * F:4 * F], bn[:, 3 * F:4 * F], vec(GAM), ALU.mult))
            link(V.tensor_tensor(Av, Av, over_tiles(bn[:, 3 * F:4 * F]), ALU.mult))
            link(V.tensor_tensor(Av, Av, over_tiles(vec(BET)), ALU.add))
            ask_act(V.tensor_scalar(H[:, :], A[:, :], 0.0, None, ALU.min))
            link(V.scalar_tensor_tensor(A[:, :], A[:, :], 0.0, H[:, :], ALU.max, ALU.add))
            link(V.scalar_tensor_tensor(X[:, :], A[:, :], -1.0, X[:, :], ALU.add, ALU.add))
            layernorm_relu().then_inc(layer_in, 1)

            def gat_out(i):
                ps = psB[:, 0:TG * 2 * F].rearrange("p (t a f) -> p t a f", a=2, f=F)
                V.tensor_copy(Av[:, bass.ds(i * TG, TG), :], ps[:, :, 0, :])
                V.tensor_copy(Rv[:, bass.ds(i * TG, TG), :], ps[:, :, 1, :])

            product_steps(G_GAT, F, gat_out)
            V.engine_nop().then_inc(table_rows, 1)
            link(V.engine_nop())
            link(V.tensor_tensor(H[:, :], A[:, :], R[:, :], ALU.add))
            link(V.scalar_tensor_tensor(H[:, :], H[:, :], SLOPE, H[:, :], ALU.mult, ALU.max))
            link(V.tensor_tensor(Hv, Hv, over_tiles(vec(ATT)), ALU.mult))
            V.memset(den[:, :], 1.0)
            link(V.tensor_reduce(mx[:, :], Hv, AX, ALU.add))
            dve.wait_ge(table_ready, 48)
            V.memset(neg, -BIG)
            for a in (psA, psB, psCD):
                V.memset(a[:, :], 0.0)
            V.memset(pr, 0.0)
            V.memset(decay[:, :], 1.0)
            V.memset(row_sum[:, :], 0.0)
            V.memset(oT, 0.0)
            for semaphore in (s_ready, sT_ready, e_ready, p_ready, neg_ready, att_sum):
                V.engine_nop().then_inc(semaphore, 1)
            V.engine_nop().then_inc(visits_init, 1)
            link(V.engine_nop())
            dve.reg_mov(visit, 0)
            for r in then:
                dve.reg_mov(r, 0)
            onehot_at, old_at, col4 = (dve.alloc_register(f"dve_{n}") for n in ("onehot_at", "old_at", "col4"))
            dve.reg_mov(onehot_at, GE)
            dve.reg_mov(old_at, 0)
            dve.reg_mov(col4, 1)

            def gat_visit(t, row):
                dve.reg_add(visit, visit, 1)
                shift(dve, then, t)
                onehot, old = ring(dve, onehot_at, GE, 4 * GE), ring(dve, old_at, GE, 2 * GE)
                if row is None:
                    V.tensor_scalar(oT[:, onehot], dst_bc[:, 0, :], -2.0, None, ALU.is_equal).then_inc(mask_ready, 1)
                else:
                    V.tensor_scalar(oT[:, onehot], row, node_no[:, bass.ds(t, 1)], None, ALU.is_equal).then_inc(mask_ready, 1)
                dve.wait_ge(s_ready, visit)
                V.tensor_scalar(sT[:, old], psA[:, old], floor[:, 0:1], None, ALU.max).then_inc(sT_ready, 1)
                dve.wait_ge(loaded_edges, 16 * 9)
                dve.wait_ge(neg_ready, visit)
                dve.wait_ge(e_ready, visit)
                V.tensor_tensor_reduce(out=em, in0=psB[:, 0:GE], in1=neg, scale=1.0,
                                       scalar=-3.0e38, op0=ALU.add, op1=ALU.max, accum_out=gmax[:, :]).then_inc(gmax_ready, 1)
                dve.wait_ge(gmax_ready, visit)
                m_t = mx[:, bass.ds(dve.snap(then[2], min_val=0, max_val=T - 1), 1)]
                V.tensor_scalar(neg_max[:, :], gmax[:, :], m_t, -1.0, ALU.max, ALU.mult).then_inc(new_max, 1)
                dve.wait_ge(new_max, visit)
                V.tensor_tensor(diff[:, :], m_t, neg_max[:, :], ALU.add).then_inc(diff_ready, 1)
                dve.wait_ge(att_sum, visit)
                u = dve.snap(then[4], min_val=0, max_val=T - 1)
                c = ring(dve, col4, 1, 4)
                l_t, o_t = den[:, bass.ds(u, 1)], Av[:, bass.ds(u, 1), :]
                V.scalar_tensor_tensor(l_t, l_t, decay[:, c], row_sum[:, c], ALU.mult, ALU.add)
                V.scalar_tensor_tensor(o_t, o_t, decay[:, c], psD[:, 0:F].unsqueeze(1), ALU.mult, ALU.add).then_inc(att_added, 1)
                dve.wait_ge(diff_ready, visit)
                V.tensor_scalar(m_t, neg_max[:, :], -1.0, None, ALU.mult).then_inc(max_kept, 1)
                turn(dve, onehot_at, GE, 4 * GE)
                turn(dve, old_at, GE, 2 * GE)
                turn(dve, col4, 1, 4)

            with dve.Fori(0, IT) as i:
                group_bounds(dve, i, regs)
                for s in range(S):
                    dve.wait_ge(bc_ready[s % SD], (i * (S // SD) + (s // SD + 1)) * 16)
                    with tiles(dve, regs, s) as t:
                        gat_visit(t, dst_bc[:, s % SD, :])
                    V.engine_nop().then_inc(bc_free[s % SD], 1)
                    give_back(s)
            with dve.Fori(0, LAG) as t:
                gat_visit(t, None)
            for s in range(LAG):
                give_back(s)
            dve.reg_add(visit, visit, 1)
            dve.wait_ge(loaded_edges, 16 * 9)
            dve.wait_ge(neg_ready, visit)
            link(V.engine_nop())
            link(V.reciprocal(s1[:, :], den[:, :]))
            link(V.tensor_tensor(Av, Av, over_features(s1[:, :]), ALU.mult))
            link(V.tensor_tensor(X[:, :], X[:, :], A[:, :], ALU.add))
            link(V.tensor_tensor(Xv, Xv, over_tiles(vec(B1)), ALU.add))
            layernorm_relu().then_inc(layer_in, 1)

            dve.reg_mov(visit, 0)

            def sum_pass():
                with dve.Fori(0, IT) as i:
                    group_bounds(dve, i, regs)
                    for s in range(S):
                        col = i * (S * J) + s * J
                        with tiles(dve, regs, s) as t:
                            dve.reg_add(visit, visit, 1)
                            V.scalar_tensor_tensor(oh16v, iota_row[:, :].unsqueeze(1).to_broadcast([P, J, P]),
                                                   tile_base[:, bass.ds(t, 1)],
                                                   dstf[:, bass.ds(col, J)].unsqueeze(2).to_broadcast([P, J, P]),
                                                   ALU.add, ALU.is_equal).then_inc(oh16_ready, 1)
                            dve.wait_ge(sum16_ready, visit)
                            V.tensor_tensor(Av[:, bass.ds(t, 1), :], Av[:, bass.ds(t, 1), :], psD[:, 0:F].unsqueeze(1), ALU.add)
                        free_slot(s)

            LINKS = 5
            with dve.Fori(0, 3) as layer:
                count = [0]

                def layer_link(ins):
                    count[0] += 1
                    ins.then_inc(layer_sem, 1)
                    dve.wait_ge(layer_sem, layer * LINKS + count[0])

                V.tensor_copy(w_cur[:, :], w_gcn[:, bass.ds(layer * F, F)]).then_inc(w_ready, 1)

                def gcn_out(i):
                    ps = psB[:, 0:TG * F].rearrange("p (t f) -> p t f", f=F)
                    V.tensor_tensor(Rv[:, bass.ds(i * TG, TG), :], ps,
                                    dinv[:, bass.ds(i * TG, TG)].unsqueeze(2).to_broadcast([P, TG, F]), ALU.mult)

                product_steps(layer * NT + G_GCN, F, gcn_out)
                V.engine_nop().then_inc(split_ask, 1)
                dve.wait_ge(split_done, layer * 2 + 1)
                V.tensor_tensor(Hv, Rv, Qv[:, :, 0, :], ALU.subtract).then_inc(split_ask, 1)
                dve.wait_ge(split_done, layer * 2 + 2)
                V.tensor_tensor(Qv[:, :, 2, :], Hv, Qv[:, :, 1, :], ALU.subtract).then_inc(table_rows, 1)
                V.memset(A[:, :], 0.0)
                sum_pass()
                layer_link(V.engine_nop())
                layer_link(V.tensor_tensor(A[:, :], A[:, :], R[:, :], ALU.add))
                layer_link(V.tensor_tensor(Av, Av, over_features(dinv[:, :]), ALU.mult))
                layer_link(V.tensor_tensor(Hv, Av, over_tiles(vecs[:, bass.ds(layer * F + GB * F, F)]), ALU.add))
                V.tensor_scalar(H[:, :], H[:, :], 0.0, None, ALU.max).then_inc(layer_in, 1)
                layer_link(V.engine_nop())
                assert count[0] == LINKS
            link(V.tensor_tensor(X[:, :], X[:, :], H[:, :], ALU.add))
            ask_act(layernorm_relu())
            ask_act(V.tensor_tensor(Rv, Hv, Qv[:, :, 0, :], ALU.subtract))
            V.tensor_tensor(Qv[:, :, 2, :], Rv, Qv[:, :, 1, :], ALU.subtract).then_inc(table_rows, 1)
            link(V.memset(A[:, :], 0.0))
            sum_pass()
            link(V.engine_nop())
            link(V.tensor_tensor(Xv, Xv, over_tiles(vec(B3)), ALU.add))
            V.tensor_tensor(Av, Av, over_features(rdeg[:, :]), ALU.mult).then_inc(layer_in, 1)

            def sage_out(i):
                at = Xv[:, bass.ds(i * TG, TG), :]
                V.tensor_tensor(at, at, psB[:, 0:TG * F].rearrange("p (t f) -> p t f", f=F), ALU.add)

            product_steps(G_SAGE, 2 * F, sage_out)
            V.engine_nop().then_inc(out_ready, 1)


_INS = ['x', 'src', 'dst', 'edge_attr_3', 'L0_gnn_W', 'L0_gnn_root', 'L0_gnn_gamma', 'L0_gnn_beta', 'L1_gnn_W_l',
        'L1_gnn_W_r', 'L1_gnn_att', 'L1_gnn_bias', 'L2_gnn_W0', 'L2_gnn_b0', 'L2_gnn_W1', 'L2_gnn_b1', 'L2_gnn_W2',
        'L2_gnn_b2', 'L3_gnn_W', 'L3_gnn_b']


def kernel(**inputs):
    import numpy as _np
    import concourse.bacc as _bacc
    from concourse import mybir as _mybir
    from concourse.bass_utils import run_bass_kernel_spmd as _run

    nc = _bacc.Bacc("TRN2", target_bir_lowering=False, num_devices=1)
    arrays, args = {}, []
    for name in _INS:
        a = _np.ascontiguousarray(inputs[name])
        arrays[f"in_{name}_dram"] = a
        args.append(nc.dram_tensor(f"in_{name}_dram", a.shape, _mybir.dt.from_np(a.dtype), kind="ExternalInput").ap())
    out = nc.dram_tensor("out_0_dram", inputs["x"].shape, _mybir.dt.float32, kind="ExternalOutput").ap()
    gnn_stack_kernel(nc, *args, out)
    r = _run(nc, [arrays], core_ids=[0])
    return r.results[0]["out_0_dram"]
```

```python
import concourse.bass as bass
from concourse import mybir
from contextlib import ExitStack


def gnn_stack_kernel(
    nc, x, src, dst, edge_attr, W0, root, gamma, beta, W_l, W_r, att, bias1,
    gW0, gb0, gW1, gb1, gW2, gb2, W3, b3, out,
):
    fp32 = mybir.dt.float32
    bf16 = mybir.dt.bfloat16
    fp32r = mybir.dt.float32r
    i32 = mybir.dt.int32
    ALU = mybir.AluOpType
    ACT = mybir.ActivationFunctionType
    AX = mybir.AxisListType.X

    P = 128
    N, F = x.shape
    E = src.shape[0]
    D = edge_attr.shape[1]
    KS = W0.shape[0]
    T = (N + P - 1) // P
    TF = N // P
    NR = N - TF * P
    J = 4
    S = 8
    SD = 4
    GE = J * P
    NG = -(-E // (GE * S)) * S
    IT = NG // S
    NB = -(-NG * J // P)
    CH = NB * P
    EB = E // (P * P)
    ER = (E - EB * P * P) // P
    EL = E - EB * P * P - ER * P
    TG = 7
    NT = T // TG
    TS = 2 * TG
    NS = T // TS
    assert TS * NS == T and NT % 2 == 0 and KS == 2 ** D and D == 3 and 2 * F == P
    BIG = 1.0e30
    EPS = 1e-5
    SLOPE = 0.2

    spline_tab = nc.dram_tensor("spline_tab", (T * P, F), fp32).ap()
    gat_tab = nc.dram_tensor("gat_tab", (T * P, 2 * F), fp32).ap()
    sum_tab = nc.dram_tensor("sum_tab", (T * P, 3 * F), bf16).ap()
    dst_rows = nc.dram_tensor("dst_rows", (CH * P,), fp32).ap()
    bounds_dram = nc.dram_tensor("bounds_dram", (NB * P // J * 2,), i32).ap()

    ctx = ExitStack()
    with ctx:
        def sb(name, shape, dt=fp32):
            return ctx.enter_context(nc.sbuf_tensor(name, shape, dt))

        def pb(name, cols):
            return ctx.enter_context(nc.psum_tensor(name, [P, cols], fp32))

        def sem(name):
            return ctx.enter_context(nc.semaphore(name))

        X = sb("X", [P, T * F])
        H = sb("H", [P, T * F])
        A = sb("A", [P, T * F])
        R = sb("R", [P, T * F])
        Q = sb("Q", [P, T * 3 * F], bf16)
        Xv, Hv, Av, Rv = (a[:, :].rearrange("p (t f) -> p t f", f=F) for a in (X, H, A, R))
        Qv = Q[:, :].rearrange("p (t s f) -> p t s f", s=3, f=F)

        srci = sb("srci", [P, CH], i32)
        dstf = sb("dstf", [P, CH])
        idx_ring = sb("idx_ring", [P, S * J], i32)
        gath = sb("gath", [P, S * J * P])
        bounds = sb("bounds", [1, NB * P // J * 2], i32)
        gath_spline = gath[:, :].rearrange("p (s j c) -> p s j c", s=S, j=J)[:, :, :, 0:F]
        gath_gat = gath[:, :].rearrange("p (s j c) -> p s j c", s=S, j=J)
        gath_sum = gath[:, :].bitcast(bf16).rearrange("p (s j c) -> p s j c", s=S, j=J)[:, :, :, 0:3 * F]

        ident = sb("ident", [P, P])
        ones = sb("ones", [P, P])
        iota_row = sb("iota_row", [P, P])
        tile_base = sb("tile_base", [P, T])
        node_no = sb("node_no", [P, T])
        pad_mask = sb("pad_mask", [P, 1])
        vecs = sb("vecs", [P, 8 * F])
        GAM, BET, ATT, B1, GB, B3 = 0, 1, 2, 3, 4, 7
        w_spline = sb("w_spline", [P, KS // 2 * F])
        w_root = sb("w_root", [F, F])
        w_gat = sb("w_gat", [F, 2 * F])
        w_gcn = sb("w_gcn", [F, 3 * F])
        w_cur = sb("w_cur", [F, F])
        w3_raw = sb("w3_raw", [F, 2 * F])
        w3 = sb("w3", [2 * F, F])
        att_col = sb("att_col", [P, 1])
        att_mat = sb("att_mat", [P, P])
        stage = sb("stage", [P, 2 * TG * P])
        hT = sb("hT", [P, 2 * TG * P])
        cnt = sb("cnt", [P, T])
        rdeg = sb("rdeg", [P, T])
        dinv = sb("dinv", [P, T])
        mx = sb("mx", [P, T])
        den = sb("den", [P, T])
        s1 = sb("s1", [P, T])
        s2 = sb("s2", [P, T])
        bn = sb("bn", [P, 4 * F])
        cmm = sb("cmm", [P, 2 * NB])
        bnd_f = sb("bnd_f", [NB, 2 * P // J])
        bnd_i = sb("bnd_i", [NB, 2 * P // J], i32)

        raw_dst = A[:, 0:NB * P].bitcast(i32).rearrange("p (b e) -> p b e", b=NB)
        raw_src = A[:, NB * P:2 * NB * P].bitcast(i32).rearrange("p (b e) -> p b e", b=NB)
        rawf_dst = A[:, 2 * NB * P:3 * NB * P].rearrange("p (b e) -> p b e", b=NB)
        raw_att = R[:, 0:NB * P * D].rearrange("p (b e) -> p b e", b=NB)
        rawf_src = H[:, 0:NB * P].rearrange("p (b e) -> p b e", b=NB)
        wmin = H[:, NB * P:2 * NB * P].rearrange("p (b e) -> p b e", b=NB)
        hat = Q[:, 0:NG * J * D * 4].bitcast(fp32).rearrange("p (c d w) -> p c d w", d=D, w=2)
        z = R[:, 0:2 * J * KS * F].rearrange("p (w j c) -> p w j c", w=2, j=J)
        o = 2 * J * KS * F
        zt = R[:, o:o + GE]
        o += GE
        hat2 = R[:, o:o + 4 * J].rearrange("p (j a b) -> p j a b", a=2, b=2)
        hat8 = R[:, o + 4 * J:o + 12 * J].rearrange("p (j a b) -> p j a b", a=2, b=4)
        Q32 = Q[:, :].bitcast(fp32)
        dst_bc = Q32[:, 0:SD * GE].rearrange("p (s e) -> p s e", s=SD)
        o = SD * GE
        neg = Q32[:, o:o + GE]
        sT = Q32[:, o + GE:o + 3 * GE]
        o += 3 * GE
        em, pr, prT = (Q32[:, o + k * GE:o + (k + 1) * GE] for k in range(3))
        floor = sb("floor", [P, 1])
        neg_max = sb("neg_max", [P, 1])
        diff = sb("diff", [P, 1])
        gmax = sb("gmax", [P, 1])
        edge_count = sb("edge_count", [P, 4])
        decay = sb("decay", [P, 4])
        row_sum = sb("row_sum", [P, 4])
        ones_r = sb("ones_r", [P, 2], fp32r)
        one_hot = sb("one_hot", [P, 4 * GE], fp32r)
        oh32r = one_hot[:, 0:GE].rearrange("p (j n) -> p j n", j=J)
        oh32 = one_hot[:, 0:GE].bitcast(fp32).rearrange("p (j n) -> p j n", j=J)
        oT = one_hot[:, :]
        oT32 = one_hot[:, :].bitcast(fp32)
        xr_hi = sb("xr_hi", [P, 2 * F], fp32r)
        xr_lo = sb("xr_lo", [P, 2 * F], fp32r)
        oh16 = sb("oh16", [P, GE], bf16)
        oh16v = oh16[:, :].rearrange("p (j n) -> p j n", j=J)

        psA = pb("psA", 1024)
        psB = pb("psB", 1024)
        psCD = pb("psCD", 1024)
        psC, psD = psCD[:, 0:512], psCD[:, 512:1024]
        psE = pb("psE", 1024)
        ps_turned, ps_product = (psA, psB), (psCD, psE)

        loaded_edges = sem("loaded_edges")
        loaded_nodes = sem("loaded_nodes")
        loaded_params = sem("loaded_params")
        raw_clear = sem("raw_clear")
        pool_const = sem("pool_const")
        pool_step = sem("pool_step")
        rows_float = sem("rows_float")
        rows_stored = sem("rows_stored")
        set_t = sem("set_t")
        set_e = sem("set_e")
        bounds_ready = sem("bounds_ready")
        bounds_stored = sem("bounds_stored")
        bounds_loaded = sem("bounds_loaded")
        link_sem = sem("link_sem")
        node_act = sem("node_act")
        node_vec = sem("node_vec")
        layer_in = sem("layer_in")
        layer_sem = sem("layer_sem")
        rows_ready = sem("rows_ready")
        high_ready = sem("high_ready")
        rest_ready = sem("rest_ready")
        middle_ready = sem("middle_ready")
        piece_split = sem("piece_split")
        oh16_ready = sem("oh16_ready")
        sum16_ready = sem("sum16_ready")
        bn_ask = sem("bn_ask")
        bn_sum = sem("bn_sum")
        table_rows = sem("table_rows")
        table_ready = sem("table_ready")
        staged = sem("staged")
        prod_t = sem("prod_t")
        prod_te = sem("prod_te")
        prod_m = sem("prod_m")
        prod_me = sem("prod_me")
        w_ready = sem("w_ready")
        idx_ready = [sem(f"idx_ready{s}") for s in range(S)]
        gathered = [sem(f"gathered{s}") for s in range(S)]
        slot_free = [sem(f"slot_free{s}") for s in range(S)]
        bc_ready = [sem(f"bc_ready{s}") for s in range(SD)]
        bc_free = [sem(f"bc_free{s}") for s in range(SD)]
        hat2_ready = sem("hat2_ready")
        hat8_ready = sem("hat8_ready")
        z_ready = sem("z_ready")
        oh_ready = [sem(f"oh_ready{j}") for j in range(J)]
        oh_used = [sem(f"oh_used{j}") for j in range(J)]
        zt_ready = sem("zt_ready")
        spline_sum = sem("spline_sum")
        spline_added = sem("spline_added")
        mask_ready = sem("mask_ready")
        xr_ready = sem("xr_ready")
        s_ready = sem("s_ready")
        sT_ready = sem("sT_ready")
        e_ready = sem("e_ready")
        neg_ready = sem("neg_ready")
        gmax_ready = sem("gmax_ready")
        new_max = sem("new_max")
        diff_ready = sem("diff_ready")
        max_kept = sem("max_kept")
        p_ready = sem("p_ready")
        pT_ready = sem("pT_ready")
        pT_moved = sem("pT_moved")
        att_sum = sem("att_sum")
        att_added = sem("att_added")
        visits_init = sem("visits_init")
        layer_done = sem("layer_done")
        out_ready = sem("out_ready")
        stored = sem("stored")

        block = ctx.enter_context(nc.Block())

        SPLINE, GAT, GCN, SAGE = 0, 1, 2, 5
        G_ROOT, G_GAT, G_GCN, G_SAGE = 0, NT, 2 * NT, 5 * NT

        def vec(k, cols=F):
            return vecs[:, k * F:k * F + cols]

        def over_tiles(ap):
            return ap.unsqueeze(1).to_broadcast([P, T, F])

        def over_features(ap):
            return ap.unsqueeze(2).to_broadcast([P, T, F])

        def wait_apart(eng, register, semaphore, target):
            eng.reg_mov(register, target)
            eng.wait_ge(loaded_edges, 16 * 9)
            eng.wait_ge(semaphore, register)

        def group_bounds(eng, i, regs):
            eng.load(regs, bounds[0:1, bass.ds(i * 2 * S, 2 * S)])

        def tiles(eng, regs, s):
            lo = eng.snap(regs[2 * s], min_val=0, max_val=T - 1)
            hi = eng.snap(regs[2 * s + 1], min_val=1, max_val=T)
            return eng.Fori(lo, hi)

        def registers(eng, name, n):
            regs = [eng.alloc_register(f"{name}{k}") for k in range(n)]
            for r in regs:
                eng.reg_mov(r, 0)
            return regs

        def shift(eng, regs, value):
            for k in range(len(regs) - 1, 0, -1):
                eng.reg_mov(regs[k], regs[k - 1])
            eng.reg_mov(regs[0], value)

        def ring(v, back, slots, stride, width=None):
            return bass.ds(((v + (slots - back) % slots) & (slots - 1)) * stride, width or stride)

        def this_visit(eng, visit):
            return eng.snap(visit, min_val=1, max_val=NG * T + LAG)

        LAG = 4

        def piece(a, c):
            return a[:, c * TS:(c + 1) * TS, :]

        @block.sync
        def _(sp):
            sp.wait_ge(raw_clear, 1)
            for raw, lst in ((raw_dst, dst), (raw_src, src)):
                full = EB * P * P
                sp.dma_start(raw[:, 0:EB, :], lst[0:full].rearrange("(b r e) -> r b e", b=EB, r=P)).then_inc(loaded_edges, 16)
                sp.dma_start(raw[0:ER, EB, :], lst[full:full + ER * P].rearrange("(r e) -> r e", e=P)).then_inc(loaded_edges, 16)
                sp.dma_start(raw[ER:ER + 1, EB, 0:EL], lst[full + ER * P:E].rearrange("(r e) -> r e", r=1)).then_inc(loaded_edges, 16)
            ea = edge_attr.rearrange("e d -> (e d)")
            full = EB * P * P * D
            sp.dma_start(raw_att[:, 0:EB, :], ea[0:full].rearrange("(b r e) -> r b e", b=EB, r=P)).then_inc(loaded_edges, 16)
            sp.dma_start(raw_att[0:ER, EB, :], ea[full:full + ER * P * D].rearrange("(r e) -> r e", r=ER)).then_inc(loaded_edges, 16)
            sp.dma_start(raw_att[ER:ER + 1, EB, 0:EL * D], ea[full + ER * P * D:E * D].rearrange("(r e) -> r e", r=1)).then_inc(loaded_edges, 16)
            sp.dma_start(Xv[:, 0:TF, :], x[0:TF * P, :].rearrange("(t p) f -> p t f", p=P)).then_inc(loaded_nodes, 16)
            sp.dma_start(Xv[0:NR, TF, :], x[TF * P:N, :]).then_inc(loaded_nodes, 16)
            sp.wait_ge(rows_float, 1)
            sp.dma_start(dst_rows.rearrange("(b r e) -> r b e", b=NB, r=P), rawf_dst).then_inc(rows_stored, 16)
            sp.wait_ge(bounds_ready, 1)
            sp.dma_start(bounds_dram.rearrange("(b g) -> b g", b=NB), bnd_i[:, :]).then_inc(bounds_stored, 16)
            sp.wait_ge(bounds_stored, 16)
            sp.dma_start(bounds[:, :], bounds_dram.rearrange("(a g) -> a g", a=1)).then_inc(bounds_loaded, 16)

            def edge_pass(done, early, with_dst=False):
                with sp.Fori(0, IT) as i:
                    for s in range(S):
                        sp.wait_ge(slot_free[s], i + (done + 1 + (early if s >= LAG else 0)))
                        sp.dma_start(idx_ring[:, s * J:(s + 1) * J],
                                     srci[:, bass.ds(i * (S * J) + s * J, J)]).then_inc(idx_ready[s], 16)
                        if with_dst:
                            sp.wait_ge(bc_free[s % SD], i * (S // SD) + (s // SD + 1))
                            row = dst_rows[bass.ds(i * (S * GE) + s * GE, GE)]
                            sp.dma_start(dst_bc[:, s % SD, :],
                                         row.rearrange("(a e) -> a e", a=1).to_broadcast([P, GE])).then_inc(bc_ready[s % SD], 16)

            sp.wait_ge(table_rows, 1)
            sp.dma_start(spline_tab.rearrange("(t p) f -> p t f", p=P), Hv).then_inc(table_ready, 16)
            edge_pass(SPLINE * IT, 1)
            sp.wait_ge(table_rows, 2)
            rows = gat_tab.rearrange("(t p) (a f) -> p t a f", p=P, a=2)
            for a in range(2):
                sp.dma_start(rows[:, :, a, :], Av).then_inc(table_ready, 16)
            sp.wait_ge(rows_stored, 16)
            edge_pass(GAT * IT, 2, with_dst=True)
            split_rows = sum_tab.rearrange("(t p) c -> p t c", p=P)
            Qrows = Q[:, :].rearrange("p (t c) -> p t c", t=T)

            def store_pieces(before):
                for c in range(NS):
                    sp.wait_ge(piece_split, before + (c + 1))
                    piece = slice(c * TS, (c + 1) * TS)
                    sp.dma_start(split_rows[:, piece, :], Qrows[:, piece, :]).then_inc(table_ready, 16)

            with sp.Fori(0, 3) as layer:
                store_pieces(layer * NS)
                edge_pass(layer * IT + GCN * IT, 2)
            store_pieces(3 * NS)
            edge_pass(SAGE * IT, 2)
            sp.wait_ge(out_ready, 1)
            sp.dma_start(out[0:TF * P, :].rearrange("(t p) f -> p t f", p=P), Xv[:, 0:TF, :]).then_inc(stored, 16)
            sp.dma_start(out[TF * P:N, :], Xv[0:NR, TF, :]).then_inc(stored, 16)
            sp.wait_ge(stored, 32)

        @block.gpsimd
        def _(pool):
            nc.gpsimd.memset(ident[:, :], 0.0).then_inc(pool_step, 1)
            nc.gpsimd.memset(ones[:, :], 1.0).then_inc(pool_step, 1)
            nc.gpsimd.iota(iota_row[:, :], [[1, P]], base=0, channel_multiplier=0,
                           allow_small_or_imprecise_dtypes=True).then_inc(pool_step, 1)
            nc.gpsimd.iota(tile_base[:, :], [[P, T]], base=0, channel_multiplier=0,
                           allow_small_or_imprecise_dtypes=True).then_inc(pool_step, 1)
            nc.gpsimd.iota(node_no[:, :], [[P, T]], base=0, channel_multiplier=1,
                           allow_small_or_imprecise_dtypes=True).then_inc(pool_step, 1)
            pool.wait_ge(pool_step, 5)
            nc.gpsimd.affine_select(out=ident[:, :], in_=ident[:, :], compare_op=ALU.not_equal, fill=1.0,
                                    base=0, pattern=[[-1, P]], channel_multiplier=1).then_inc(pool_const, 1)

            pool_count = pool.alloc_register("pool_count")

            def edge_pass(table, dest, done, tables_stored):
                wait_apart(pool, pool_count, table_ready, tables_stored)
                with pool.Fori(0, IT) as i:
                    for s in range(S):
                        wait_apart(pool, pool_count, idx_ready[s], (i + done + 1) * 16)
                        for j in range(J):
                            nc.gpsimd.indirect_dma_start(
                                out=dest[:, s, j, :], out_offset=None, in_=table,
                                in_offset=bass.IndirectOffsetOnAxis(ap=idx_ring[:, s * J + j:s * J + j + 1], axis=0),
                            ).then_inc(gathered[s], 16)

            edge_pass(spline_tab, gath_spline, SPLINE * IT, 16)
            edge_pass(gat_tab, gath_gat, GAT * IT, 48)
            with pool.Fori(0, 3) as layer:
                edge_pass(sum_tab, gath_sum, layer * IT + GCN * IT, layer * (16 * NS) + (48 + 16 * NS))
            edge_pass(sum_tab, gath_sum, SAGE * IT, 48 + 4 * 16 * NS)

        @block.scalar
        def _(act):
            def bc(v, n=F):
                return v.rearrange("(a f) -> a f", a=1).to_broadcast([P, n])

            for k, v in ((GAM, gamma), (BET, beta), (ATT, att), (B1, bias1), (GB, gb0), (GB + 1, gb1), (GB + 2, gb2), (B3, b3)):
                act.dma_start(vec(k), bc(v)).then_inc(loaded_params, 16)
            act.dma_start(w_spline[:, :].rearrange("p (k o) -> p k o", o=F),
                          W0.rearrange("(k s) c o -> (s c) k o", s=2)).then_inc(loaded_params, 16)
            act.dma_start(w_root[:, :], root).then_inc(loaded_params, 16)
            act.dma_start(w_gat[:, 0:F], W_l).then_inc(loaded_params, 16)
            act.dma_start(w_gat[:, F:2 * F], W_r).then_inc(loaded_params, 16)
            for k, w in enumerate((gW0, gW1, gW2)):
                act.dma_start(w_gcn[:, k * F:(k + 1) * F], w).then_inc(loaded_params, 16)
            act.dma_start(w3_raw[:, :], W3).then_inc(loaded_params, 16)
            for a in range(2):
                act.dma_start(att_col[a * F:(a + 1) * F, :], att.rearrange("(f a) -> f a", a=1)).then_inc(loaded_params, 16)

            steps = [0]

            def node_step(src_ap, dst_ap, func):
                steps[0] += 1
                act.wait_ge(node_vec, steps[0])
                nc.scalar.activation(dst_ap, src_ap, func).then_inc(node_act, 1)

            def layernorm_steps():
                node_step(R[:, :], H[:, :], ACT.Square)
                node_step(s2[:, :], s2[:, :], ACT.Sqrt)

            def split_steps(rows, rest, before, pieces):
                act.wait_ge(rows_ready, before + 1)
                for c in range(NS + 1):
                    if c < NS:
                        nc.scalar.activation(piece(Qv[:, :, 0, :], c), piece(rows, c), ACT.Copy).then_inc(high_ready, 1)
                    if c > 0:
                        act.wait_ge(rest_ready, pieces + c)
                        nc.scalar.activation(piece(Qv[:, :, 1, :], c - 1), piece(rest, c - 1), ACT.Copy).then_inc(middle_ready, 1)

            def stage_tiles(parts, first, func=ACT.Copy):
                K = sum(p.shape[2] for p in parts)
                with act.Fori(0, NT // 2) as i:
                    for w in range(2):
                        to = stage[:, w * TG * P:w * TG * P + TG * K].rearrange("p (t k) -> p t k", k=K)
                        act.wait_ge(prod_t, i * 2 + (first + w + 1))
                        at = 0
                        for part in parts:
                            k = part.shape[2]
                            nc.scalar.activation(to[:, :, at:at + k], part[:, bass.ds(i * (2 * TG) + w * TG, TG), :],
                                                 func).then_inc(staged, 1)
                            at += k

            regs = [act.alloc_register(f"act_bound{k}") for k in range(2 * S)]
            visit = act.alloc_register("act_visit")
            act.reg_mov(visit, 0)

            layernorm_steps()
            act.wait_ge(bounds_loaded, 16)

            def spline_visit():
                act.reg_add(visit, visit, 1)
                v = this_visit(act, visit)
                act.wait_ge(spline_sum, visit)
                nc.scalar.activation(edge_count[:, ring(v, 1, 4, 1)], psE[:, ring(v, 1, 2, GE, 1)], ACT.Copy)
                nc.scalar.activation(zt, psA[:, ring(v, 1, 2, GE)], ACT.Copy).then_inc(zt_ready, 1)

            with act.Fori(0, IT) as i:
                group_bounds(act, i, regs)
                for s in range(S):
                    with tiles(act, regs, s):
                        spline_visit()
            with act.Fori(0, 2):
                spline_visit()
            node_step(s2[:, :], s2[:, :], ACT.Sqrt)
            stage_tiles([Hv], G_ROOT)
            node_step(A[:, :], H[:, :], ACT.Square)
            node_step(bn[:, 3 * F:4 * F], bn[:, 3 * F:4 * F], ACT.Sqrt)
            node_step(H[:, :], H[:, :], ACT.Exp)
            layernorm_steps()
            act.wait_ge(layer_in, 1)
            stage_tiles([Hv], G_GAT)
            node_step(R[:, :], H[:, :].bitcast(fp32r), ACT.Copy)
            act.reg_mov(visit, 0)

            def gat_visit(t):
                act.reg_add(visit, visit, 1)
                v = this_visit(act, visit)
                act.wait_ge(mask_ready, visit)
                act.wait_ge(s_ready, visit)
                for part, rows in ((xr_hi, Hv), (xr_lo, Rv)):
                    nc.scalar.activation(part[:, :].rearrange("p (a f) -> p a f", a=2),
                                         rows[:, bass.ds(t, 1), :].to_broadcast([P, 2, F]), ACT.Copy).then_inc(xr_ready, 1)
                act.wait_ge(pT_ready, visit)
                nc.scalar.activation(prT, psC[:, 0:GE], ACT.Copy).then_inc(pT_moved, 1)
                act.wait_ge(diff_ready, visit)
                c = ring(v, 2, 4, 1)
                nc.scalar.activation(decay[:, c], diff[:, :], ACT.Exp)
                nc.scalar.activation(pr, em, ACT.Exp, bias=neg_max[:, :], accum_out=row_sum[:, c]).then_inc(p_ready, 1)
                nc.scalar.activation(neg, oT32[:, ring(v, 1, 4, GE)], ACT.Copy, bias=-BIG, scale=BIG).then_inc(neg_ready, 1)

            with act.Fori(0, IT) as i:
                group_bounds(act, i, regs)
                for s in range(S):
                    with tiles(act, regs, s) as t:
                        gat_visit(t)
            with act.Fori(0, LAG) as t:
                gat_visit(t)
            layernorm_steps()
            with act.Fori(0, 3) as layer:
                act.wait_ge(layer_in, layer + 2)
                stage_tiles([Hv], layer * NT + G_GCN, ACT.Relu)
                split_steps(Rv, Hv, layer, layer * NS)
            layernorm_steps()
            split_steps(Hv, Rv, 3, 3 * NS)
            act.wait_ge(layer_in, 6)
            stage_tiles([Av, Hv], G_SAGE)

        @block.tensor
        def _(pe):
            pe.wait_ge(pool_const, 1)
            pe.wait_ge(rows_float, 1)
            jobs = [(rawf_dst[:, b, :], P) for b in range(NB)] + [(rawf_src[:, b, :], P) for b in range(NB)]
            for d in range(D):
                jobs += [(raw_att[:, b, d::D], P) for b in range(NB)]
            for n, (rows, k) in enumerate(jobs):
                if n >= 2:
                    pe.wait_ge(set_e, n - 1)
                nc.tensor.transpose(psA[:, (n % 2) * 512:(n % 2) * 512 + P], rows, ident[:, :]).then_inc(set_t, 1)
            nc.tensor.transpose(psB[0:NB, 0:P], cmm[:, 0:NB], ident[:, :]).then_inc(set_t, 1)
            nc.tensor.transpose(psB[0:NB, 512:512 + P], cmm[:, NB:2 * NB], ident[:, :]).then_inc(set_t, 1)
            pe.wait_ge(loaded_params, 16 * 18)
            nc.tensor.transpose(psC[:, 0:F], w3_raw[:, :], ident[0:F, 0:F]).then_inc(set_t, 1)

            pe_count = pe.alloc_register("pe_count")

            def product(K, weights, NW, first, parts=1, staged_before=None):
                with pe.Fori(0, NT // 2) as i:
                    for w in range(2):
                        wait_apart(pe, pe_count, staged, i * (2 * parts) + (staged_before + (w + 1) * parts))
                        for k in range(TG):
                            at = w * TG * P + k * K
                            ins = nc.tensor.transpose(ps_turned[w][0:K, k * P:(k + 1) * P], stage[:, at:at + K], ident[:, :])
                        ins.then_inc(prod_t, 1)
                    for w in range(2):
                        pe.wait_ge(prod_te, i * 2 + (first + w + 1))
                        for k in range(TG):
                            at = w * TG * P + k * P
                            ins = nc.tensor.matmul(ps_product[w][:, k * NW:(k + 1) * NW], hT[0:K, at:at + P], weights,
                                                   start=True, stop=True)
                        ins.then_inc(prod_m, 1)

            regs = [pe.alloc_register(f"pe_bound{k}") for k in range(2 * S)]
            visit = pe.alloc_register("pe_visit")
            pe.reg_mov(visit, 0)
            pe.wait_ge(bounds_loaded, 16)

            def spline_visit(w):
                pe.reg_add(visit, visit, 1)
                v = this_visit(pe, visit)
                count = ring(v, 0, 2, GE, 2)
                for k in range(KS // 2):
                    block = psA[:, bass.ds((v & 1) * GE + k * P, P)]
                    for j in range(J):
                        if k == 0:
                            pe.wait_ge(oh_ready[j], visit)
                        nc.tensor.matmul(block, z[:, w, j, k * P:(k + 1) * P], oh32[:, j, :],
                                         start=(j == 0), stop=(j == J - 1))
                        if k == KS // 2 - 1:
                            nc.tensor.matmul(psE[:, count], oh32r[:, j, :], ones_r[:, :], start=(j == 0),
                                             stop=(j == J - 1)).then_inc(oh_used[j], 1)
                pe.wait_ge(zt_ready, visit)
                for k in range(KS // 2):
                    ins = nc.tensor.matmul(psCD[:, ring(v, 1, 2, GE, F)], zt[:, k * P:(k + 1) * P], w_spline[:, k * F:(k + 1) * F],
                                           start=(k == 0), stop=(k == KS // 2 - 1))
                ins.then_inc(spline_sum, 1)

            pe.wait_ge(visits_init, 1)
            with pe.Fori(0, IT) as i:
                group_bounds(pe, i, regs)
                for s in range(S):
                    pe.wait_ge(z_ready, i * S + (s + 1))
                    with tiles(pe, regs, s):
                        spline_visit(s % 2)
            with pe.Fori(0, 2):
                spline_visit(0)
            product(F, w_root[:, :], F, G_ROOT, staged_before=0)
            for n in range(2):
                pe.wait_ge(bn_ask, n + 1)
                nc.tensor.matmul(psC[:, 0:F], ones[:, :], bn[:, n * F:(n + 1) * F], start=True, stop=True).then_inc(bn_sum, 1)
            product(F, w_gat[:, :], 2 * F, G_GAT, staged_before=NT)
            pe.reg_mov(visit, 0)
            next_visit = pe.alloc_register("pe_next_visit")
            twice = pe.alloc_register("pe_twice")
            pe.reg_mov(twice, 0)
            slots = registers(pe, "pe_slot", LAG)

            def gat_visit(s):
                pe.reg_add(visit, visit, 1)
                pe.reg_add(next_visit, visit, 1)
                pe.reg_add(twice, twice, 2)
                shift(pe, slots, s * J * P)
                v = this_visit(pe, visit)
                pair = ring(v, 0, 2, GE)
                pe.wait_ge(p_ready, visit)
                for j in range(J):
                    ins = nc.tensor.transpose(psC[:, j * P:(j + 1) * P], pr[:, j * P:(j + 1) * P], ident[:, :])
                ins.then_inc(pT_ready, 1)
                pe.wait_ge(xr_ready, twice)
                pe.wait_ge(sT_ready, visit)
                onehot = oT[:, ring(v, 0, 4, GE)]
                nc.tensor.matmul(psA[:, pair], xr_hi[:, :], onehot, start=True, stop=False)
                nc.tensor.matmul(psA[:, pair], xr_lo[:, :], onehot, start=False, stop=False)
                for j in range(J):
                    ins = nc.tensor.matmul(psA[:, bass.ds((v & 1) * GE + j * P, P)], gath_gat[:, s, j, :], ident[:, :],
                                           start=False, stop=(j == J - 1))
                ins.then_inc(s_ready, 1)
                pe.wait_ge(sT_ready, next_visit)
                pe.wait_ge(gmax_ready, visit)
                nc.tensor.matmul(psB[:, 0:GE], att_mat[:, :], sT[:, ring(v, 1, 2, GE)],
                                 start=True, stop=True).then_inc(e_ready, 1)
                pe.wait_ge(pT_moved, visit)
                pe.wait_ge(att_added, visit)
                for j in range(J):
                    o = pe.snap(slots[3], min_val=0, max_val=(S - 1) * J * P)
                    ins = nc.tensor.matmul(psD[:, 0:F], prT[:, j * P:(j + 1) * P], gath[:, bass.ds(o + j * P, F)],
                                           start=(j == 0), stop=(j == J - 1))
                ins.then_inc(att_sum, 1)

            pe.wait_ge(visits_init, 2)
            with pe.Fori(0, IT) as i:
                group_bounds(pe, i, regs)
                for s in range(S):
                    pe.wait_ge(gathered[s], (i + (GAT * IT + 1)) * (16 * J))
                    with tiles(pe, regs, s):
                        gat_visit(s)
            with pe.Fori(0, LAG):
                gat_visit(0)

            pe.reg_mov(visit, 0)

            def sum_pass(done):
                with pe.Fori(0, IT) as i:
                    group_bounds(pe, i, regs)
                    for s in range(S):
                        pe.wait_ge(gathered[s], (i + done + 1) * (16 * J))
                        with tiles(pe, regs, s):
                            pe.reg_add(visit, visit, 1)
                            pe.wait_ge(oh16_ready, visit)
                            for j in range(J):
                                for part in range(3):
                                    ins = nc.tensor.matmul(psD[:, 0:F], oh16v[:, j, :], gath_sum[:, s, j, part * F:(part + 1) * F],
                                                           start=(j == 0 and part == 0), stop=(j == J - 1 and part == 2))
                            ins.then_inc(sum16_ready, 1)

            with pe.Fori(0, 3) as layer:
                wait_apart(pe, pe_count, w_ready, layer + 1)
                product(F, w_cur[:, :], F, layer * NT + G_GCN, staged_before=layer * NT + 2 * NT)
                sum_pass(layer * IT + GCN * IT)
            sum_pass(SAGE * IT)
            product(2 * F, w3[:, :], F, G_SAGE, parts=2, staged_before=5 * NT)

        @block.vector
        def _(dve):
            chain = [0]

            def link(ins):
                chain[0] += 1
                ins.then_inc(link_sem, 1)
                dve.wait_ge(link_sem, chain[0])

            V = nc.vector

            V.memset(raw_dst[:, EB, :], -1)
            V.memset(raw_src[:, EB, :], 0)
            V.memset(Xv[:, TF, :], 0.0)
            V.memset(raw_att[:, EB, :], 0.0).then_inc(raw_clear, 1)
            dve.wait_ge(loaded_edges, 16 * 9)
            V.tensor_copy(rawf_src, raw_src)
            link(V.tensor_copy(rawf_dst, raw_dst))
            link(V.tensor_scalar(wmin, rawf_dst, 0.0, 2.0 * N, ALU.is_lt, ALU.mult))
            link(V.tensor_tensor(wmin, wmin, rawf_dst, ALU.add))
            V.tensor_reduce(cmm[:, 0:NB], wmin, AX, ALU.min)
            V.tensor_reduce(cmm[:, NB:2 * NB], rawf_dst, AX, ALU.max).then_inc(rows_float, 1)
            for n in range((2 + D) * NB):
                b = n % NB
                ps = psA[:, (n % 2) * 512:(n % 2) * 512 + P]
                at = slice(b * P, (b + 1) * P)
                dve.wait_ge(set_t, n + 1)
                if n < NB:
                    V.tensor_copy(dstf[:, at], ps).then_inc(set_e, 1)
                elif n < 2 * NB:
                    V.tensor_copy(srci[:, at], ps).then_inc(set_e, 1)
                else:
                    w = min(P, NG * J - b * P)
                    V.tensor_scalar(hat[:, b * P:b * P + w, n // NB - 2, 1], ps[:, 0:w], 0.0, 1.0, ALU.max, ALU.min).then_inc(set_e, 1)
            dve.wait_ge(set_e, (2 + D) * NB)
            link(V.tensor_scalar(hat[:, :, :, 0], hat[:, :, :, 1], -1.0, 1.0, ALU.mult, ALU.add))
            dve.wait_ge(set_t, (2 + D) * NB + 2)
            bf = bnd_f[:, :].rearrange("b (g w) -> b g w", w=2)
            bi = bnd_i[:, :].rearrange("b (g w) -> b g w", w=2)
            V.tensor_reduce(bf[:, :, 0], psB[0:NB, 0:P].rearrange("b (g j) -> b g j", j=J), AX, ALU.min)
            link(V.tensor_reduce(bf[:, :, 1], psB[0:NB, 512:512 + P].rearrange("b (g j) -> b g j", j=J), AX, ALU.max))
            link(V.tensor_scalar(bf[:, :, 0], bf[:, :, 0], float(T * P - 1), None, ALU.min))
            link(V.tensor_tensor(bf[:, :, 1], bf[:, :, 1], bf[:, :, 0], ALU.max))
            link(V.tensor_copy(bnd_i[:, :], bnd_f[:, :]))
            link(V.tensor_scalar(bnd_i[:, :], bnd_i[:, :], 7, None, ALU.arith_shift_right))
            V.tensor_scalar(bi[:, :, 1], bi[:, :, 1], 1, None, ALU.add).then_inc(bounds_ready, 1)
            dve.wait_ge(set_t, (2 + D) * NB + 3)
            V.tensor_copy(w3[:, :], psC[:, 0:F])
            V.memset(floor[0:F, :], 0.0)
            V.memset(floor[F:P, :], -3.0e38)
            V.tensor_scalar(att_mat[0:F, :], att_col[0:F, 0:1].to_broadcast([F, P]), 1.0 - SLOPE, None, ALU.mult)
            V.tensor_scalar(att_mat[F:P, :], att_col[F:P, 0:1].to_broadcast([F, P]), SLOPE, None, ALU.mult)
            V.tensor_scalar(pad_mask[:, :], node_no[:, T - 1:T], float(N), None, ALU.is_lt)
            link(V.memset(cnt[:, :], 0.0))
            for semaphore in slot_free + bc_free + [prod_t, prod_t]:
                V.engine_nop().then_inc(semaphore, 1)

            asked = [0]

            def ask_act(ins):
                asked[0] += 1
                ins.then_inc(node_vec, 1)
                dve.wait_ge(node_act, asked[0])

            def layernorm_relu():
                link(V.tensor_reduce(s1[:, :], Xv, AX, ALU.add))
                link(V.tensor_scalar(s1[:, :], s1[:, :], 1.0 / F, None, ALU.mult))
                ask_act(V.tensor_tensor(Rv, Xv, over_features(s1[:, :]), ALU.subtract))
                link(V.tensor_reduce(s2[:, :], Hv, AX, ALU.add))
                ask_act(V.tensor_scalar(s2[:, :], s2[:, :], 1.0 / F, EPS, ALU.mult, ALU.add))
                link(V.reciprocal(s2[:, :], s2[:, :]))
                return V.scalar_tensor_tensor(Hv, Rv, 0.0, over_features(s2[:, :]), ALU.max, ALU.mult)

            regs = [dve.alloc_register(f"dve_bound{k}") for k in range(2 * S)]
            visit = dve.alloc_register("dve_visit")
            dve.reg_mov(visit, 0)

            def free_slot(s):
                V.engine_nop().then_inc(slot_free[s], 1)

            dve.wait_ge(loaded_nodes, 32)
            layernorm_relu().then_inc(table_rows, 1)
            dve.wait_ge(rows_stored, 16)
            link(V.memset(A[:, :], 0.0))

            dve.wait_ge(bounds_loaded, 16)
            V.memset(edge_count[:, :], 0.0)
            V.tensor_copy(ones_r[:, :], ones[:, 0:2])
            for a in (psA, psCD, psE):
                V.memset(a[:, :], 0.0)
            for semaphore in oh_used + [spline_sum, spline_added]:
                V.engine_nop().then_inc(semaphore, 1)
            V.engine_nop().then_inc(visits_init, 1)
            then = registers(dve, "dve_tile", 5)

            def spline_visit(t, chunk_col):
                dve.reg_add(visit, visit, 1)
                shift(dve, then, t)
                for j in range(J):
                    dve.wait_ge(oh_used[j], visit)
                    if chunk_col is None:
                        V.tensor_scalar(oh32r[:, j, :], iota_row[:, :], 0.0, None, ALU.mult).then_inc(oh_ready[j], 1)
                    else:
                        V.tensor_scalar(oh32r[:, j, :], iota_row[:, :], tile_base[:, bass.ds(t, 1)],
                                        dstf[:, bass.ds(chunk_col + j, 1)], ALU.add, ALU.is_equal).then_inc(oh_ready[j], 1)
                dve.wait_ge(spline_sum, visit)
                dve.wait_ge(spline_added, visit)
                u = dve.snap(then[2], min_val=0, max_val=T - 1)
                v = this_visit(dve, visit)
                o_t, c_t = Av[:, bass.ds(u, 1), :], cnt[:, bass.ds(u, 1)]
                V.tensor_tensor(o_t, o_t, psCD[:, ring(v, 2, 2, GE, F)].unsqueeze(1), ALU.add)
                V.tensor_tensor(c_t, c_t, edge_count[:, ring(v, 2, 4, 1)], ALU.add).then_inc(spline_added, 1)

            def give_back(s):
                free_slot((s - LAG) % S)

            with dve.Fori(0, IT) as i:
                group_bounds(dve, i, regs)
                for s in range(S):
                    col = i * (S * J) + s * J
                    h3 = hat[:, bass.ds(col, J), :, :]
                    V.tensor_tensor(hat2, h3[:, :, 1, :].unsqueeze(3).to_broadcast([P, J, 2, 2]),
                                    h3[:, :, 0, :].unsqueeze(2).to_broadcast([P, J, 2, 2]), ALU.mult).then_inc(hat2_ready, 1)
                    dve.wait_ge(hat2_ready, i * S + (s + 1))
                    V.tensor_tensor(hat8, h3[:, :, 2, :].unsqueeze(3).to_broadcast([P, J, 2, 4]),
                                    hat2.rearrange("p j a b -> p j (a b)").unsqueeze(2).to_broadcast([P, J, 2, 4]),
                                    ALU.mult).then_inc(hat8_ready, 1)
                    dve.wait_ge(hat8_ready, i * S + (s + 1))
                    dve.wait_ge(gathered[s], (i + 1) * (16 * J))
                    V.tensor_tensor(z[:, s % 2, :, :].rearrange("p j (k f) -> p j k f", f=F),
                                    gath_spline[:, s, :, :].unsqueeze(2).to_broadcast([P, J, KS, F]),
                                    hat8.rearrange("p j a b -> p j (a b)").unsqueeze(3).to_broadcast([P, J, KS, F]),
                                    ALU.mult).then_inc(z_ready, 1)
                    with tiles(dve, regs, s) as t:
                        spline_visit(t, col)
                    give_back(s)
            with dve.Fori(0, 2) as t:
                spline_visit(t, None)
            for s in range(LAG):
                give_back(s)

            def product_steps(first, K, evac):
                with dve.Fori(0, NT // 2) as i:
                    for w in range(2):
                        dve.wait_ge(prod_t, i * 2 + (first + w + 3))
                        V.tensor_copy(hT[0:K, w * TG * P:(w + 1) * TG * P], ps_turned[w][0:K, 0:TG * P]).then_inc(prod_te, 1)
                    for w in range(2):
                        dve.wait_ge(prod_m, i * 2 + (first + w + 1))
                        evac(bass.ds(i * (2 * TG) + w * TG, TG), ps_product[w])

            link(V.engine_nop())
            link(V.tensor_scalar(s1[:, :], cnt[:, :], 1.0, None, ALU.max))
            V.reciprocal(rdeg[:, :], s1[:, :])
            ask_act(V.tensor_scalar(s2[:, :], cnt[:, :], 1.0, None, ALU.add))
            V.reciprocal(dinv[:, :], s2[:, :])
            link(V.engine_nop())
            link(V.tensor_tensor(Av, Av, over_features(rdeg[:, :]), ALU.mult))

            def root_out(tiles, ps):
                at = Av[:, tiles, :]
                V.tensor_tensor(at, at, ps[:, 0:TG * F].rearrange("p (t f) -> p t f", f=F), ALU.add)

            product_steps(G_ROOT, F, root_out)
            link(V.engine_nop())
            V.tensor_reduce(bn[:, 0:F], Av.rearrange("p t f -> p f t"), AX, ALU.add).then_inc(bn_ask, 1)
            dve.wait_ge(bn_sum, 1)
            link(V.tensor_scalar(bn[:, 2 * F:3 * F], psC[:, 0:F], 1.0 / N, None, ALU.mult))
            link(V.tensor_tensor(Av, Av, over_tiles(bn[:, 2 * F:3 * F]), ALU.subtract))
            V.tensor_scalar(Av[:, T - 1, :], Av[:, T - 1, :], pad_mask[:, 0:1], None, ALU.mult)
            ask_act(V.engine_nop())
            V.tensor_reduce(bn[:, F:2 * F], Hv.rearrange("p t f -> p f t"), AX, ALU.add).then_inc(bn_ask, 1)
            dve.wait_ge(bn_sum, 2)
            ask_act(V.tensor_scalar(bn[:, 3 * F:4 * F], psC[:, 0:F], 1.0 / N, EPS, ALU.mult, ALU.add))
            link(V.reciprocal(bn[:, 3 * F:4 * F], bn[:, 3 * F:4 * F]))
            dve.wait_ge(loaded_params, 16 * 18)
            link(V.tensor_tensor(bn[:, 3 * F:4 * F], bn[:, 3 * F:4 * F], vec(GAM), ALU.mult))
            link(V.tensor_tensor(Av, Av, over_tiles(bn[:, 3 * F:4 * F]), ALU.mult))
            link(V.tensor_tensor(Av, Av, over_tiles(vec(BET)), ALU.add))
            ask_act(V.tensor_scalar(H[:, :], A[:, :], 0.0, None, ALU.min))
            link(V.scalar_tensor_tensor(A[:, :], A[:, :], 0.0, H[:, :], ALU.max, ALU.add))
            link(V.scalar_tensor_tensor(X[:, :], A[:, :], -1.0, X[:, :], ALU.add, ALU.add))
            layernorm_relu().then_inc(layer_in, 1)

            def gat_out(tiles, ps):
                ps = ps[:, 0:TG * 2 * F].rearrange("p (t a f) -> p t a f", a=2, f=F)
                V.tensor_copy(Av[:, tiles, :], ps[:, :, 0, :])
                V.tensor_copy(Rv[:, tiles, :], ps[:, :, 1, :])

            product_steps(G_GAT, F, gat_out)
            V.engine_nop().then_inc(table_rows, 1)
            link(V.engine_nop())
            link(V.tensor_tensor(H[:, :], A[:, :], R[:, :], ALU.add))
            link(V.scalar_tensor_tensor(H[:, :], H[:, :], SLOPE, H[:, :], ALU.mult, ALU.max))
            link(V.tensor_tensor(Hv, Hv, over_tiles(vec(ATT)), ALU.mult))
            V.memset(den[:, :], 1.0)
            link(V.tensor_reduce(mx[:, :], Hv, AX, ALU.add))
            ask_act(V.engine_nop())
            link(V.tensor_tensor(R[:, :], R[:, :], H[:, :], ALU.subtract))
            link(V.tensor_tensor(Xv, Xv, over_tiles(vec(B1)), ALU.add))
            dve.wait_ge(table_ready, 48)
            V.memset(neg, -BIG)
            for a in (psA, psB, psCD):
                V.memset(a[:, :], 0.0)
            V.memset(pr, 0.0)
            V.memset(decay[:, :], 1.0)
            V.memset(row_sum[:, :], 0.0)
            V.tensor_scalar(oT.rearrange("p (a n) -> p a n", n=P), iota_row[:, :].unsqueeze(1).to_broadcast([P, 4 * J, P]),
                            0.0, None, ALU.mult)
            for semaphore in (s_ready, sT_ready, e_ready, p_ready, neg_ready, att_sum):
                V.engine_nop().then_inc(semaphore, 1)
            V.engine_nop().then_inc(visits_init, 1)
            link(V.engine_nop())
            dve.reg_mov(visit, 0)
            for r in then:
                dve.reg_mov(r, 0)

            def gat_visit(t, row):
                dve.reg_add(visit, visit, 1)
                shift(dve, then, t)
                v = this_visit(dve, visit)
                onehot, old = ring(v, 0, 4, GE), ring(v, 1, 2, GE)
                if row is None:
                    V.tensor_scalar(oT[:, onehot], dst_bc[:, 0, :], -2.0, None, ALU.is_equal).then_inc(mask_ready, 1)
                else:
                    V.tensor_scalar(oT[:, onehot], row, node_no[:, bass.ds(t, 1)], None, ALU.is_equal).then_inc(mask_ready, 1)
                dve.wait_ge(loaded_edges, 16 * 9)
                dve.wait_ge(neg_ready, visit)
                dve.wait_ge(e_ready, visit)
                V.tensor_tensor_reduce(out=em, in0=psB[:, 0:GE], in1=neg, scale=1.0,
                                       scalar=-3.0e38, op0=ALU.add, op1=ALU.max, accum_out=gmax[:, :]).then_inc(gmax_ready, 1)
                dve.wait_ge(s_ready, visit)
                V.tensor_scalar(sT[:, old], psA[:, old], floor[:, 0:1], None, ALU.max).then_inc(sT_ready, 1)
                dve.wait_ge(gmax_ready, visit)
                m_t = mx[:, bass.ds(dve.snap(then[2], min_val=0, max_val=T - 1), 1)]
                V.tensor_scalar(neg_max[:, :], gmax[:, :], m_t, -1.0, ALU.max, ALU.mult).then_inc(new_max, 1)
                dve.wait_ge(att_sum, visit)
                u = dve.snap(then[4], min_val=0, max_val=T - 1)
                c = ring(v, 4, 4, 1)
                l_t, o_t = den[:, bass.ds(u, 1)], Av[:, bass.ds(u, 1), :]
                V.scalar_tensor_tensor(l_t, l_t, decay[:, c], row_sum[:, c], ALU.mult, ALU.add)
                dve.wait_ge(new_max, visit)
                V.tensor_tensor(diff[:, :], m_t, neg_max[:, :], ALU.add).then_inc(diff_ready, 1)
                V.scalar_tensor_tensor(o_t, o_t, decay[:, c], psD[:, 0:F].unsqueeze(1), ALU.mult, ALU.add).then_inc(att_added, 1)
                dve.wait_ge(diff_ready, visit)
                V.tensor_scalar(m_t, neg_max[:, :], -1.0, None, ALU.mult).then_inc(max_kept, 1)

            with dve.Fori(0, IT) as i:
                group_bounds(dve, i, regs)
                for s in range(S):
                    dve.wait_ge(bc_ready[s % SD], (i * (S // SD) + (s // SD + 1)) * 16)
                    with tiles(dve, regs, s) as t:
                        gat_visit(t, dst_bc[:, s % SD, :])
                    V.engine_nop().then_inc(bc_free[s % SD], 1)
                    give_back(s)
            with dve.Fori(0, LAG) as t:
                gat_visit(t, None)
            for s in range(LAG):
                give_back(s)
            dve.reg_add(visit, visit, 1)
            dve.wait_ge(loaded_edges, 16 * 9)
            dve.wait_ge(neg_ready, visit)
            link(V.engine_nop())
            link(V.reciprocal(s1[:, :], den[:, :]))
            link(V.tensor_tensor(Av, Av, over_features(s1[:, :]), ALU.mult))
            link(V.tensor_tensor(X[:, :], X[:, :], A[:, :], ALU.add))
            layernorm_relu().then_inc(layer_in, 1)

            dve.reg_mov(visit, 0)

            def sum_pass():
                with dve.Fori(0, IT) as i:
                    group_bounds(dve, i, regs)
                    for s in range(S):
                        col = i * (S * J) + s * J
                        with tiles(dve, regs, s) as t:
                            dve.reg_add(visit, visit, 1)
                            V.scalar_tensor_tensor(oh16v, iota_row[:, :].unsqueeze(1).to_broadcast([P, J, P]),
                                                   tile_base[:, bass.ds(t, 1)],
                                                   dstf[:, bass.ds(col, J)].unsqueeze(2).to_broadcast([P, J, P]),
                                                   ALU.add, ALU.is_equal).then_inc(oh16_ready, 1)
                            dve.wait_ge(sum16_ready, visit)
                            V.tensor_tensor(Av[:, bass.ds(t, 1), :], Av[:, bass.ds(t, 1), :], psD[:, 0:F].unsqueeze(1), ALU.add)
                        free_slot(s)

            def split_rows(rows, rest, pieces):
                for c in range(NS + 1):
                    if c < NS:
                        dve.wait_ge(high_ready, pieces + (c + 1))
                        V.tensor_tensor(piece(rest, c), piece(rows, c), piece(Qv[:, :, 0, :], c), ALU.subtract).then_inc(rest_ready, 1)
                    if c > 0:
                        dve.wait_ge(middle_ready, pieces + c)
                        V.tensor_tensor(piece(Qv[:, :, 2, :], c - 1), piece(rest, c - 1), piece(Qv[:, :, 1, :], c - 1),
                                        ALU.subtract).then_inc(piece_split, 1)

            LINKS = 5
            with dve.Fori(0, 3) as layer:
                count = [0]

                def layer_link(ins):
                    count[0] += 1
                    ins.then_inc(layer_sem, 1)
                    dve.wait_ge(layer_sem, layer * LINKS + count[0])

                V.tensor_copy(w_cur[:, :], w_gcn[:, bass.ds(layer * F, F)]).then_inc(w_ready, 1)

                def gcn_out(tiles, ps):
                    ps = ps[:, 0:TG * F].rearrange("p (t f) -> p t f", f=F)
                    V.tensor_tensor(Rv[:, tiles, :], ps,
                                    dinv[:, tiles].unsqueeze(2).to_broadcast([P, TG, F]), ALU.mult)

                product_steps(layer * NT + G_GCN, F, gcn_out)
                V.engine_nop().then_inc(rows_ready, 1)
                layer_link(V.engine_nop())
                layer_link(V.tensor_copy(A[:, :], R[:, :]))
                split_rows(Rv, Hv, layer * NS)
                sum_pass()
                layer_link(V.engine_nop())
                layer_link(V.tensor_tensor(Av, Av, over_features(dinv[:, :]), ALU.mult))
                V.tensor_tensor(Hv, Av, over_tiles(vecs[:, bass.ds(layer * F + GB * F, F)]), ALU.add).then_inc(layer_in, 1)
                layer_link(V.engine_nop())
                assert count[0] == LINKS
            link(V.scalar_tensor_tensor(X[:, :], H[:, :], 0.0, X[:, :], ALU.max, ALU.add))
            layernorm_relu().then_inc(rows_ready, 1)
            link(V.engine_nop())
            split_rows(Hv, Rv, 3 * NS)
            V.tensor_tensor(Xv, Xv, over_tiles(vec(B3)), ALU.add)
            link(V.memset(A[:, :], 0.0))
            sum_pass()
            link(V.engine_nop())
            V.tensor_tensor(Av, Av, over_features(rdeg[:, :]), ALU.mult).then_inc(layer_in, 1)

            def sage_out(tiles, ps):
                at = Xv[:, tiles, :]
                V.tensor_tensor(at, at, ps[:, 0:TG * F].rearrange("p (t f) -> p t f", f=F), ALU.add)

            product_steps(G_SAGE, 2 * F, sage_out)
            V.engine_nop().then_inc(out_ready, 1)


_INS = ['x', 'src', 'dst', 'edge_attr_3', 'L0_gnn_W', 'L0_gnn_root', 'L0_gnn_gamma', 'L0_gnn_beta', 'L1_gnn_W_l',
        'L1_gnn_W_r', 'L1_gnn_att', 'L1_gnn_bias', 'L2_gnn_W0', 'L2_gnn_b0', 'L2_gnn_W1', 'L2_gnn_b1', 'L2_gnn_W2',
        'L2_gnn_b2', 'L3_gnn_W', 'L3_gnn_b']


def kernel(**inputs):
    import numpy as _np
    import concourse.bacc as _bacc
    from concourse import mybir as _mybir
    from concourse.bass_utils import run_bass_kernel_spmd as _run

    nc = _bacc.Bacc("TRN2", target_bir_lowering=False, num_devices=1)
    arrays, args = {}, []
    for name in _INS:
        a = _np.ascontiguousarray(inputs[name])
        arrays[f"in_{name}_dram"] = a
        args.append(nc.dram_tensor(f"in_{name}_dram", a.shape, _mybir.dt.from_np(a.dtype), kind="ExternalInput").ap())
    out = nc.dram_tensor("out_0_dram", inputs["x"].shape, _mybir.dt.float32, kind="ExternalOutput").ap()
    gnn_stack_kernel(nc, *args, out)
    r = _run(nc, [arrays], core_ids=[0])
    return r.results[0]["out_0_dram"]
```
